# Optimizing a Trainium2 kernel written in Bass

```python
import numpy as np
import jax
import jax.numpy as jnp

def _softmax(x, axis=-1):
    return jax.nn.softmax(x, axis=axis)

def _gelu(x):
    return jax.nn.gelu(x, approximate=True)

def _silu(x):
    return jax.nn.silu(x)

def _sigmoid(x):
    return jax.nn.sigmoid(x)

def _layernorm(x, axis=-1, eps=1e-05):
    m = jnp.mean(x, axis=axis, keepdims=True)
    v = jnp.var(x, axis=axis, keepdims=True)
    return (x - m) / jnp.sqrt(v + eps)

def _scatter_add(tgt, idx, src, axis=0):
    return tgt.at[idx].add(src)

def _segment_sum(src, seg, n):
    return jax.ops.segment_sum(src, seg, n)
kernel_name = 'mk_seq_preln_d1_jaxref_r8_b6a4eb'

def setup_inputs(seed: int=0):
    np.random.seed(seed)
    _w = jnp.asarray

    def _L0_attn_setup():
        import jax, jax.numpy as jnp
        import numpy as np
        K_HEADS = 16
        key = jax.random.key(seed)
        k1, k2 = jax.random.split(key)
        z = jax.random.normal(k1, (2, 256, 128), dtype=jnp.float32)
        W_qkv = jax.random.normal(k2, (384, 128), dtype=jnp.float32) * (1.0 / np.sqrt(128))
        return {'z': z, 'W_qkv': W_qkv}
    _L0_attn_in = _L0_attn_setup()

    def _L0_ffn_setup():
        import jax, jax.numpy as jnp
        import numpy as np
        TOP_K = 2
        CAPACITY = 512
        EPS = 1e-06
        W_SCALE = 0.02

        def _rms(x, w):
            return x * jax.lax.rsqrt(jnp.mean(x * x, axis=-1, keepdims=True) + EPS) * w
        key = jax.random.key(seed)
        ks = jax.random.split(key, 8)
        B, S, H, F, E = (8, 512, 128, 256, 8)
        F4 = F // 4
        return {'hidden_states': jax.random.normal(ks[0], (B, S, H), jnp.float32), 'Wr': jax.random.normal(ks[1], (H, E), jnp.float32) * W_SCALE, 'norm_w': jnp.ones((E, H), jnp.float32), 'Wg': jax.random.normal(ks[2], (E, H, F), jnp.float32) * W_SCALE, 'Wu': jax.random.normal(ks[3], (E, H, F), jnp.float32) * W_SCALE, 'Wd': jax.random.normal(ks[4], (E, F, H), jnp.float32) * W_SCALE, 'f_norm': jnp.ones((H,), jnp.float32), 'fWg': jax.random.normal(ks[5], (H, F4), jnp.float32) * W_SCALE, 'fWu': jax.random.normal(ks[6], (H, F4), jnp.float32) * W_SCALE, 'fWd': jax.random.normal(ks[7], (F4, H), jnp.float32) * W_SCALE}
    _L0_ffn_in = _L0_ffn_setup()
    _d = {'L0_attn_z': _L0_attn_in['z'], 'L0_attn_W_qkv': _L0_attn_in['W_qkv'], 'L0_ffn_Wr': _L0_ffn_in['Wr'], 'L0_ffn_norm_w': _L0_ffn_in['norm_w'], 'L0_ffn_Wg': _L0_ffn_in['Wg'], 'L0_ffn_Wu': _L0_ffn_in['Wu'], 'L0_ffn_Wd': _L0_ffn_in['Wd'], 'L0_ffn_f_norm': _L0_ffn_in['f_norm'], 'L0_ffn_fWg': _L0_ffn_in['fWg'], 'L0_ffn_fWu': _L0_ffn_in['fWu'], 'L0_ffn_fWd': _L0_ffn_in['fWd']}
    _x0 = _d['L0_attn_z']
    _d['L0_attn_z'] = jax.random.normal(jax.random.fold_in(jax.random.key(seed), 1), (4, 1024, 128), dtype=_x0.dtype)
    del _x0
    return _d

def reference(L0_attn_z, L0_attn_W_qkv, L0_ffn_Wr, L0_ffn_norm_w, L0_ffn_Wg, L0_ffn_Wu, L0_ffn_Wd, L0_ffn_f_norm, L0_ffn_fWg, L0_ffn_fWu, L0_ffn_fWd):

    def _L0_attn_ref(z, W_qkv):
        import jax, jax.numpy as jnp
        import numpy as np
        K_HEADS = 16
        b, n, D = z.shape
        k = K_HEADS
        Dh = D // k
        qkv = jnp.einsum('bnd,ed->bne', z, W_qkv)
        qkv = qkv.reshape(b, n, k, 3, Dh).transpose(3, 0, 2, 1, 4)
        q, kk, v = (qkv[0], qkv[1], qkv[2])
        scale = 1.0 / jnp.sqrt(jnp.asarray(Dh, dtype=z.dtype))
        scores = jnp.einsum('bhnd,bhmd->bhnm', q, kk) * scale
        A = jax.nn.softmax(scores, axis=-1)
        out = jnp.einsum('bhnm,bhmd->bhnd', A, v)
        return out.transpose(0, 2, 1, 3).reshape(b, n, D)

    def _L0_ffn_ref(hidden_states, Wr, norm_w, Wg, Wu, Wd, f_norm, fWg, fWu, fWd):
        import jax, jax.numpy as jnp
        import numpy as np
        TOP_K = 2
        CAPACITY = 512
        EPS = 1e-06
        W_SCALE = 0.02

        def _rms(x, w):
            return x * jax.lax.rsqrt(jnp.mean(x * x, axis=-1, keepdims=True) + EPS) * w
        B, S, H = hidden_states.shape
        E = Wr.shape[1]
        N = B * S
        x = hidden_states.reshape(N, H)
        probs = jax.nn.softmax(x @ Wr, axis=-1)
        w_topk, e_topk = jax.lax.top_k(probs, TOP_K)
        e_flat = e_topk.reshape(-1)
        oh = jax.nn.one_hot(e_flat, E, dtype=jnp.int32)
        pos = jnp.take_along_axis(jnp.cumsum(oh, axis=0) - 1, e_flat[:, None], axis=1)[:, 0]
        keep = pos < CAPACITY
        x_rep = jnp.repeat(x, TOP_K, axis=0)
        buf = jnp.zeros((E, CAPACITY, H), x.dtype).at[e_flat, pos].set(x_rep, mode='drop')
        h = _rms(buf, norm_w[:, None, :])
        gate = jax.nn.gelu(jnp.einsum('ech,ehf->ecf', h, Wg), approximate=False)
        up = jnp.einsum('ech,ehf->ecf', h, Wu)
        buf_out = jnp.einsum('ecf,efh->ech', gate * up, Wd) + buf
        exp_out = buf_out[e_flat, jnp.minimum(pos, CAPACITY - 1)]
        contrib = w_topk.reshape(-1)[:, None] * exp_out * keep[:, None].astype(x.dtype)
        combined = x + contrib.reshape(N, TOP_K, H).sum(axis=1)
        overflow = (~keep).reshape(N, TOP_K).any(axis=1)
        fh = _rms(x, f_norm)
        fout = jax.nn.gelu(fh @ fWg, approximate=False) * (fh @ fWu) @ fWd + x
        out = jnp.where(overflow[:, None], fout, combined)
        return out.reshape(B, S, H)
    x = L0_attn_z
    x = x + _L0_attn_ref(_layernorm(x, axis=-1), L0_attn_W_qkv)
    x = x + _L0_ffn_ref(_layernorm(x, axis=-1), L0_ffn_Wr, L0_ffn_norm_w, L0_ffn_Wg, L0_ffn_Wu, L0_ffn_Wd, L0_ffn_f_norm, L0_ffn_fWg, L0_ffn_fWu, L0_ffn_fWd)
    return x

_drawn_inputs = setup_inputs


def setup_inputs(seed=0):
    import zlib

    import numpy as np

    out = dict(_drawn_inputs(seed))
    spreads = {'L0_ffn_norm_w': (1.0, 0.6), 'L0_ffn_f_norm': (1.0, 0.6)}
    factors = {'L0_ffn_Wr': 2.97,
     'L0_ffn_Wg': 8.0,
     'L0_ffn_Wu': 8.0,
     'L0_ffn_Wd': 8.0,
     'L0_ffn_fWg': 8.0,
     'L0_ffn_fWu': 8.0,
     'L0_ffn_fWd': 8.0}
    for name, (base, spread) in spreads.items():
        noise = np.random.default_rng([zlib.crc32(name.encode()), seed]).standard_normal(out[name].shape)
        drawn = base * np.exp(spread * noise) if base else spread * noise
        out[name] = jnp.asarray(drawn.astype(out[name].dtype))
    for name, factor in factors.items():
        out[name] = (out[name] * factor).astype(out[name].dtype)
    return out
```

```python
from contextlib import ExitStack

import concourse.bass as bass
from concourse import mybir

F32 = mybir.dt.float32
BF16 = mybir.dt.bfloat16
U32 = mybir.dt.uint32
ALU = mybir.AluOpType
ACT = mybir.ActivationFunctionType
AX = mybir.AxisListType

P = 128
B, S, D = 4, 1024, 128
N = B * S
H, DH = 16, 8
NPAIR = B * H // 2
TB = S // P
NT = N // P
HALF = 512
NPART = 3
PROD = NPART * NPART * DH
SHIFT = 96
KROWS = SHIFT + NPART
QBUF = 4
PRING = 4
E = 8
CAP = 512
CT = CAP // P
F = 256
FT = F // P
F4 = 64
RW = E + 2 * F4
LN_EPS = 1e-5
RMS_EPS = 1e-6
SOFTMAX_SCALE = float(DH) ** -0.5
FAR = 1 << 16


def wait_apart(eng, semaphore, value, passed):
    eng.wait_ge(semaphore, value)
    eng.sem_inc(passed, 1)


class Chain:

    def __init__(self, eng, sem):
        self.eng, self.sem, self.base, self.k, self.it, self.per = eng, sem, 0, 0, None, 0

    def loop(self, it, per):
        self.it, self.per, self.k = it, per, 0

    def end(self, times):
        assert self.k == self.per, self.k
        self.base += times * self.per
        self.it, self.k = None, 0

    def __call__(self, ins):
        self.k += 1
        ins.then_inc(self.sem, 1)
        if self.it is None:
            self.eng.wait_ge(self.sem, self.base + self.k)
        else:
            self.eng.wait_ge(self.sem, self.it * self.per + (self.base + self.k))


def attention_moe(nc, z, W_qkv, Wr, norm_w, Wg, Wu, Wd, f_norm, fWg, fWu, fWd, out, debug=None):
    with ExitStack() as ctx:
        def sb(name, shape, dt, c=ctx):
            return c.enter_context(nc.sbuf_tensor(name, shape, dt))

        def sem(name, c=ctx):
            return c.enter_context(nc.semaphore(name))

        q_parts = nc.dram_tensor("q_parts", (NPART, NPAIR * 2 * DH, S), BF16, kind="Internal").ap()
        k_parts = nc.dram_tensor("k_parts", (NPART, NPAIR * 2 * DH, S), BF16, kind="Internal").ap()
        slots_in = nc.dram_tensor("slots_in", (E * CAP, D), F32, kind="Internal").ap()
        slots_out = nc.dram_tensor("slots_out", (E * CAP, D), F32, kind="Internal").ap()

        x = sb("x", [P, NT, D], F32)
        v_all = sb("v_all", [P, NPAIR, TB, 2, DH + 1], F32)
        att = sb("att", [P, NPAIR, 2, TB, DH], F32)
        ident = sb("ident", [P, P], F32)
        identb = sb("identb", [P, P], BF16)

        phase_qkv(nc, z, W_qkv, q_parts, k_parts, slots_in, x, v_all, ident, identb)
        phase_attention(nc, q_parts, k_parts, v_all, att, identb)
        if debug == "att":
            with nc.semaphore("dbg") as dbg, nc.Block() as block:
                @block.sync
                def _(sp):
                    sp.dma_start(out.rearrange("b (t p) d -> p (b t) d", p=P), att[:, :].rearrange("p a b c d -> p (a b c d)").rearrange("p (t d) -> p t d", d=D)).then_inc(dbg, 16)
                    sp.wait_ge(dbg, 16)
            return
        phase_moe(nc, Wr, norm_w, Wg, Wu, Wd, f_norm, fWg, fWu, fWd, slots_in, slots_out, x, att,
                  ident, identb, out)


def phase_qkv(nc, z, W_qkv, q_parts, k_parts, slots_in, x, v_all, ident, identb):
    with ExitStack() as ctx:
        def sb(name, shape, dt):
            return ctx.enter_context(nc.sbuf_tensor(name, shape, dt))

        def ps(name, shape, dt):
            return ctx.enter_context(nc.psum_tensor(name, shape, dt))

        def sem(name):
            return ctx.enter_context(nc.semaphore(name))

        w_rows = sb("w_rows", [P, 3, D], F32)
        wT = sb("wT", [P, 3, H, DH], F32)
        zn = sb("zn", [P, TB, D], F32)
        zT = sb("zT", [P, S], F32)
        stats = sb("stats", [P, TB, 6], F32)
        mv = sb("mv", [P, TB, 2], F32)
        veps = sb("veps", [P, TB], F32)
        power = sb("power", [P, TB], F32)
        rstd = sb("rstd", [P, TB], F32)
        shift = sb("shift", [P, TB], F32)
        part = sb("part", [P, 2, NPART, S], BF16)
        rest = sb("rest", [P, 2, S], F32)
        zeros = sb("zeros", [P, 8, D], F32)

        ps_T = ps("ps_T", [P, 2, HALF], F32)
        ps_qk = ps("ps_qk", [P, 2, 2, HALF], F32)
        ps_v = ps("ps_v", [P, 2, HALF], F32)

        x_in = sem("x_in")
        w_in = sem("w_in")
        masks = sem("masks")
        ones_set = sem("ones_set")
        zeroed = sem("zeroed")
        slots_zeroed = sem("slots_zeroed")
        dve_own = sem("dve_own")
        act_own = sem("act_own")
        wT_ps = sem("wT_ps")
        wT_ready = sem("wT_ready")
        stats_ready = sem("stats_ready")
        var_ready = sem("var_ready")
        rstd_ready = sem("rstd_ready")
        shift_ready = sem("shift_ready")
        zn_ready = sem("zn_ready")
        zT_ps = sem("zT_ps")
        zT_ready = sem("zT_ready")
        qkv_ps = sem("qkv_ps")
        hi_ready = sem("hi_ready")
        rest_ready = sem("rest_ready")
        mid_ready = sem("mid_ready")
        lo_ready = sem("lo_ready")
        v_ready = sem("v_ready")
        parts_out = sem("parts_out")

        block = ctx.enter_context(nc.Block())

        @block.sync
        def _(sp):
            for b in range(B):
                sp.dma_start(x[:, b * TB:(b + 1) * TB, :], z[b].rearrange("(t p) d -> p t d", p=P)).then_inc(x_in, 16)
                if b == 0:
                    sp.dma_start(w_rows[:, :, :], W_qkv.rearrange("(c p) d -> p c d", p=P)).then_inc(w_in, 16)
            sp.wait_ge(zeroed, 1)
            for c in range(E * CAP // (8 * P)):
                sp.dma_start(slots_in[c * 8 * P:(c + 1) * 8 * P, :].rearrange("(p r) d -> p r d", p=P),
                             zeros[:, :, :]).then_inc(slots_zeroed, 16)
            with sp.Fori(0, B) as b:
                for qk, store in enumerate((q_parts, k_parts)):
                    sp.wait_ge(lo_ready, b * 2 + (qk + 1))
                    for i in range(NPART):
                        sp.dma_start(store[i, bass.ds(b * P, P), :], part[:, qk, i, :]).then_inc(parts_out, 16)
            sp.wait_ge(parts_out, B * 2 * NPART * 16)
            sp.wait_ge(slots_zeroed, E * CAP // (8 * P) * 16)

        @block.gpsimd
        def _(pool):
            pool.memset(ident[:, :], 0.0).then_inc(masks, 1)
            pool.memset(identb[:, :], 0.0).then_inc(masks, 1)
            pool.wait_ge(masks, 2)
            for m in (ident, identb):
                pool.affine_select(out=m[:, :], in_=m[:, :], compare_op=ALU.not_equal, fill=1.0, base=0,
                                   pattern=[[-1, P]], channel_multiplier=1).then_inc(masks, 1)
            pool.memset(power[:, :], -0.5).then_inc(masks, 1)
            pool.memset(zeros[:, :, :], 0.0).then_inc(zeroed, 1)
            pool.memset(v_all[:, :, :, :, :], 1.0).then_inc(ones_set, 1)
            pool.wait_ge(masks, 5)
            with pool.Fori(0, B) as b:
                pool.wait_ge(var_ready, b + 1)
                pool.tensor_tensor(rstd[:, :], veps[:, :], power[:, :], ALU.pow).then_inc(rstd_ready, 1)

        @block.scalar
        def _(act):
            own = Chain(act, act_own)
            with act.Fori(0, B) as b:
                own.loop(b, 4)
                act.wait_ge(shift_ready, b + 1)
                for t in range(TB):
                    ins = act.activation(zn[:, t, :], x[:, bass.ds(b * TB + t, 1), :], ACT.Identity,
                                         bias=shift[:, t:t + 1], scale=rstd[:, t:t + 1])
                ins.then_inc(zn_ready, 1)
                act.wait_ge(zT_ps, b + 1)
                own(act.activation(zT[:, :], ps_T[:, :, :], ACT.Copy))
                act.sem_inc(zT_ready, 1)
                for qk in range(2):
                    act.wait_ge(qkv_ps, b * 3 + (qk + 1))
                    act.wait_ge(parts_out, b * (2 * NPART * 16))
                    own(act.activation(part[:, qk, 0, :], ps_qk[:, qk, :, :], ACT.Copy))
                    act.sem_inc(hi_ready, 1)
                for qk in range(2):
                    act.wait_ge(rest_ready, b * 2 + (qk + 1))
                    ins = act.activation(part[:, qk, 1, :], rest[:, qk, :], ACT.Copy)
                    ins.then_inc(mid_ready, 1)
                act.wait_ge(qkv_ps, b * 3 + 3)
                act.wait_ge(ones_set, 1)
                for t in range(TB):
                    ins = act.activation(
                        v_all[:, bass.ds(b * (H // 2), H // 2), t, :, 0:DH],
                        ps_v[:, t // 4, (t % 4) * P:(t % 4 + 1) * P].rearrange("p (m h d) -> p m h d", h=2, d=DH),
                        ACT.Copy)
                own(ins)
                act.sem_inc(v_ready, 1)
            own.end(B)

        @block.vector
        def _(dve):
            own = Chain(dve, dve_own)
            dve.wait_ge(wT_ps, 1)
            for c in range(3):
                ins = dve.tensor_copy(wT[:, c, :, :], ps_T[:, 0, 0:3 * P].rearrange(
                    "p (h c d) -> p c h d", c=3, d=DH)[:, c, :, :])
            ins.then_inc(wT_ready, 1)
            dve.wait_ge(x_in, 16 * B)
            with dve.Fori(0, B) as b:
                own.loop(b, 5)
                for t in range(TB):
                    ins = dve.bn_stats(stats[:, t, :], x[:, bass.ds(b * TB + t, 1), :])
                own(ins)
                dve.sem_inc(stats_ready, 1)
                for t in range(TB):
                    ins = dve.bn_aggr(mv[:, t, :], stats[:, t, :])
                own(ins)
                dve.tensor_scalar(veps[:, :], mv[:, :, 1], LN_EPS, None, ALU.add).then_inc(var_ready, 1)
                dve.wait_ge(rstd_ready, b + 1)
                dve.wait_ge(zn_ready, b)
                dve.scalar_tensor_tensor(out=shift[:, :], in0=mv[:, :, 0], scalar=-1.0, in1=rstd[:, :],
                                         op0=ALU.mult, op1=ALU.mult).then_inc(shift_ready, 1)
                for qk in range(2):
                    dve.wait_ge(hi_ready, b * 2 + (qk + 1))
                    own(dve.tensor_tensor(rest[:, qk, :], ps_qk[:, qk, :, :].rearrange("p a n -> p (a n)"),
                                          part[:, qk, 0, :], ALU.subtract))
                    dve.sem_inc(rest_ready, 1)
                for qk in range(2):
                    dve.wait_ge(mid_ready, b * 2 + (qk + 1))
                    ins = dve.tensor_tensor(part[:, qk, 2, :], rest[:, qk, :], part[:, qk, 1, :], ALU.subtract)
                    if qk == 1:
                        own(ins)
                        dve.sem_inc(lo_ready, 2)
            own.end(B)

        @block.tensor
        def _(pe):
            pe.wait_ge(w_in, 16)
            pe.wait_ge(masks, 4)
            for c in range(3):
                ins = pe.transpose(ps_T[:, 0, c * P:(c + 1) * P], w_rows[:, c, :], ident[:, :])
            ins.then_inc(wT_ps, 1)
            pe.wait_ge(wT_ready, 1)
            with pe.Fori(0, B) as b:
                pe.wait_ge(zn_ready, b + 1)
                pe.wait_ge(zT_ready, b)
                for t in range(TB):
                    ins = pe.transpose(ps_T[:, t // 4, (t % 4) * P:(t % 4 + 1) * P], zn[:, t, :], ident[:, :])
                ins.then_inc(zT_ps, 1)
                pe.wait_ge(zT_ready, b + 1)
                pe.wait_ge(rest_ready, b * 2)
                for qk in range(2):
                    for n in range(2):
                        ins = pe.matmul(ps_qk[:, qk, n, :], wT[:, qk, :, :].rearrange("p h d -> p (h d)"),
                                        zT[:, n * HALF:(n + 1) * HALF], start=True, stop=True)
                    ins.then_inc(qkv_ps, 1)
                pe.wait_ge(v_ready, b)
                for t in range(TB):
                    ins = pe.matmul(ps_v[:, t // 4, (t % 4) * P:(t % 4 + 1) * P], zT[:, t * P:(t + 1) * P],
                                    wT[:, 2, :, :].rearrange("p h d -> p (h d)"), start=True, stop=True)
                ins.then_inc(qkv_ps, 1)


def phase_attention(nc, q_parts, k_parts, v_all, att, identb):
    with ExitStack() as ctx:
        def sb(name, shape, dt):
            return ctx.enter_context(nc.sbuf_tensor(name, shape, dt))

        def ps(name, shape, dt):
            return ctx.enter_context(nc.psum_tensor(name, shape, dt))

        def sem(name):
            return ctx.enter_context(nc.semaphore(name))

        qo = [sb(f"qo{u}", [P, 2, S], BF16) for u in range(QBUF)]
        ko = [sb(f"ko{u}", [P, 2, S], BF16) for u in range(QBUF)]
        vb = sb("vb", [P, 2, TB, 2, DH + 1], F32)
        prob = sb("prob", [P, PRING, 4, HALF], F32)
        avs = sb("avs", [P, HALF], F32)
        nmax = sb("nmax", [P, 2, 2 * TB], F32)
        nrest = sb("nrest", [P, 2, 2 * TB], F32)
        nparts = sb("nparts", [P, 2, NPART, TB], BF16)
        shift_rows = sb("shift_rows", [2 * NPART * TB, P], BF16)
        rden = sb("rden", [P, TB, 2], F32)
        pick = sb("pick", [P, 4, DH + 1], F32)

        ps_s = ps("ps_s", [P, 2, S], F32)
        ps_t = ps("ps_t", [P, 2, HALF], F32)
        ps_av = ps("ps_av", [P, HALF], F32)
        ps_m = ps("ps_m", [P, HALF], F32)
        M_NM = ps_m[0:2 * NPART * TB, 0:P // 2].bitcast(BF16)
        M_AV = ps_m[:, 128:128 + 4 * 4 * (DH + 1)].rearrange("p (c j i) -> p c j i", c=4, j=4)

        loads = [sem(f"loads{u}") for u in range(QBUF)]
        shifts_in = [sem(f"shifts_in{u}") for u in range(QBUF)]
        buffers_set = sem("buffers_set")
        pick_set = sem("pick_set")
        scores_ready = sem("scores_ready")
        scores_reduced = sem("scores_reduced")
        keyed_ready = sem("keyed_ready")
        prob_ready = sem("prob_ready")
        av_done = sem("av_done")
        av_copied = sem("av_copied")
        v_ready = sem("v_ready")
        nparts_ready = sem("nparts_ready")
        misc_ready = sem("misc_ready")
        result_taken = sem("result_taken")
        rows_copied = sem("rows_copied")
        pool_own = sem("pool_own")
        passed = sem("passed")
        rden_ready = sem("rden_ready")
        av_cleared = sem("av_cleared")

        block = ctx.enter_context(nc.Block())
        FIRST, LAST = 1, NPAIR - 4

        def steps(eng, step):
            for s in range(-2, FIRST):
                step(s, s % QBUF, s // QBUF)
            with eng.Fori(0, (LAST - FIRST + 1) // QBUF) as i:
                for u in range(QBUF):
                    step(i * QBUF + (FIRST + u), (FIRST + u) % QBUF, i + (FIRST + u) // QBUF)
            for s in range(LAST + 1, NPAIR + 1):
                step(s, s % QBUF, s // QBUF)

        def has(s, offset):
            return not isinstance(s, int) or 0 <= s + offset < NPAIR

        def at_least(eng, semaphore, value):
            if not isinstance(value, int) or value > 0:
                eng.wait_ge(semaphore, value)

        @block.sync
        def _(sp):
            def load(pair, u):
                for hd in range(2):
                    rows = bass.ds(pair * (2 * DH) + hd * DH, DH)
                    for i in range(NPART):
                        r = i * NPART * DH
                        sp.dma_start(qo[u][r:r + NPART * DH, hd, :],
                                     q_parts[i:i + 1, rows, :].broadcast_to((NPART, DH, S))).then_inc(loads[u], 16)
                        sp.dma_start(ko[u][r:r + NPART * DH, hd, :], k_parts[:, rows, :]).then_inc(loads[u], 16)

            def step(s, u, rnd):
                if isinstance(s, int) and s == -2:
                    sp.wait_ge(buffers_set, 2 * QBUF + 1)
                    for q in range(3):
                        load(q, q)
                if has(s, 3) and not (isinstance(s, int) and s + 3 < 3):
                    at_least(sp, keyed_ready, s * (4 * TB))
                    load(s + 3, (u + 3) % QBUF)
                if has(s, 1):
                    sp.wait_ge(rows_copied, s + 2)
                    w = (u + 1) % QBUF
                    for hd in range(2):
                        sp.dma_start(qo[w][SHIFT:SHIFT + NPART, hd, :],
                                     shift_rows[hd * NPART * TB:(hd + 1) * NPART * TB, :]).then_inc(shifts_in[w], 16)
            steps(sp, step)

        @block.gpsimd
        def _(pool):
            pool.memset(pick[:, :, :], 0.0).then_inc(pick_set, 1)
            pool.wait_ge(pick_set, 1)
            pool.affine_select(out=pick[:, :, :], in_=pick[:, :, :], compare_op=ALU.not_equal, fill=1.0, base=0,
                               pattern=[[-32, 4], [-1, DH + 1]], channel_multiplier=1).then_inc(pick_set, 1)
            own = Chain(pool, pool_own)

            def step(s, u, rnd):
                if has(s, 1):
                    if not isinstance(s, int) or s > 0:
                        wait_apart(pool, av_done, s * TB, passed)
                    pool.tensor_copy(vb[:, (u + 1) % 2, :, :, :], v_all[:, bass.ds(s + 1, 1), :, :, :]).then_inc(v_ready, 1)
                if has(s, 2):
                    pool.wait_ge(scores_reduced, s * (2 * TB) + 3 * 2 * TB)
                    if not isinstance(s, int) or s > -2:
                        wait_apart(pool, misc_ready, s + 2, passed)
                    m = nmax[:, u % 2, :].rearrange("p (h t) -> p h t", h=2)
                    r = nrest[:, :, :].rearrange("p a (h t) -> p a h t", h=2)
                    for ins in (lambda: pool.tensor_copy(nparts[:, :, 0, :], m),
                                lambda: pool.tensor_tensor(r[:, 0], m, nparts[:, :, 0, :], ALU.subtract),
                                lambda: pool.tensor_copy(nparts[:, :, 1, :], r[:, 0]),
                                lambda: pool.tensor_tensor(r[:, 1], r[:, 0], nparts[:, :, 1, :], ALU.subtract)):
                        ins().then_inc(pool_own, 1)
                        own.k += 1
                        wait_apart(pool, pool_own, s * 4 + (8 + (own.k - 1) % 4 + 1), passed)
                    pool.tensor_copy(nparts[:, :, 2, :], r[:, 1]).then_inc(nparts_ready, 1)
            steps(pool, step)

        @block.scalar
        def _(act):
            def step(s, u, rnd):
                def copy_av():
                    if has(s, -1):
                        act.wait_ge(av_done, s * TB)
                        at_least(act, misc_ready, s)
                        act.activation(avs[:, :], ps_av[:, :], ACT.Copy).then_inc(av_copied, 1)
                if has(s, 0):
                    for t in range(TB):
                        if not isinstance(s, int) or TB * s + t - PRING >= 0:
                            act.wait_ge(av_done, s * TB + (t - PRING + 1))
                        for j in range(4):
                            if t == 0 and j == 3:
                                copy_av()
                            act.wait_ge(keyed_ready, s * (4 * TB) + (4 * t + j + 1))
                            act.activation(prob[:, t % PRING, j, :], ps_t[:, j % 2, :], ACT.Exp,
                                           scale=SOFTMAX_SCALE).then_inc(prob_ready, 1)
                else:
                    copy_av()
            steps(act, step)

        @block.vector
        def _(dve):
            for u in range(QBUF):
                dve.memset(qo[u][:, :, :], 0.0).then_inc(buffers_set, 1)
                dve.memset(ko[u][0:SHIFT, :, :], 0.0)
                dve.memset(ko[u][SHIFT:P, :, :], 1.0).then_inc(buffers_set, 1)
            dve.memset(ps_av[:, :], 0.0).then_inc(buffers_set, 1)

            def misc(s, u):
                dve.wait_ge(misc_ready, s + 2)
                if has(s, 1):
                    if not isinstance(s, int) or s >= 0:
                        dve.wait_ge(shifts_in[u], last_round * 32 + 32)
                    ins = dve.tensor_copy(shift_rows[:, :], M_NM)
                    ins.then_inc(rows_copied, 1)
                if has(s, -1):
                    dve.reciprocal(rden4,
                                   M_AV[:, :, :, DH]).then_inc(rden_ready, 1)
                    dve.wait_ge(rden_ready, s)
                    for hd in range(2):
                        for half in range(2):
                            j = 2 * hd + half
                            ins = dve.tensor_tensor(
                                att[:, bass.ds(s - 1, 1), hd, 4 * half:4 * half + 4, :],
                                M_AV[:, :, j, 0:DH],
                                rden4[:, :, j:j + 1].broadcast_to((P, 4, DH)), ALU.mult)
                    ins.then_inc(result_taken, 1)

            rden4 = rden[:, :, :].rearrange("p t h -> p (t h)").rearrange("p (c j) -> p c j", j=4)
            last_round = 0

            def step(s, u, rnd):
                nonlocal last_round
                last_round = rnd
                if has(s, 2):
                    at_least(dve, nparts_ready, s + 1 if not isinstance(s, int) or s > 0 else 0)
                    for k in range(2 * TB):
                        if k == 6 and not (isinstance(s, int) and s < -1):
                            misc(s, u)
                        dve.wait_ge(scores_ready, s * (2 * TB) + (4 * TB + k + 1))
                        dve.tensor_reduce(nmax[:, u % 2, k:k + 1], ps_s[:, k % 2, :], AX.X, ALU.max,
                                          negate=True).then_inc(scores_reduced, 1)
                else:
                    misc(s, u)
            steps(dve, step)

        @block.tensor
        def _(pe):
            pe.wait_ge(pick_set, 2)

            def scores_turn(s, u, k):
                w = (u + 2) % QBUF
                hd, t = k // TB, k % TB
                if not isinstance(s, int) or s > -2 or k >= 2:
                    pe.wait_ge(scores_reduced, s * (2 * TB) + (4 * TB + k - 1))
                for n in range(2):
                    ins = pe.matmul(ps_s[:, k % 2, n * HALF:(n + 1) * HALF], qo[w][0:SHIFT, hd, t * P:(t + 1) * P],
                                    ko[w][0:SHIFT, hd, n * HALF:(n + 1) * HALF], start=True, stop=True)
                ins.then_inc(scores_ready, 1)

            def keyed(s, u, t, j):
                hd, half = j // 2, j % 2
                if not isinstance(s, int) or s > 0 or 4 * t + j >= 2:
                    pe.wait_ge(prob_ready, s * (4 * TB) + (4 * t + j - 1))
                pe.matmul(ps_t[:, j % 2, :], ko[u][0:KROWS, hd, t * P:(t + 1) * P],
                          qo[u][0:KROWS, hd, half * HALF:(half + 1) * HALF], start=True, stop=True).then_inc(keyed_ready, 1)

            def values(s, u, t):
                pe.wait_ge(prob_ready, s * (4 * TB) + (4 * t + 4))
                if t == 0:
                    pe.wait_ge(v_ready, s + 1)
                    at_least(pe, av_copied, s)
                for j in range(4):
                    ins = pe.matmul(ps_av[32 * j:32 * j + DH + 1, :], vb[:, u % 2, t, j // 2, :],
                                    prob[:, t % PRING, j, :], start=(t == 0), stop=(t == TB - 1))
                ins.then_inc(av_done, 1)

            def misc(s, u):
                if has(s, 0):
                    at_least(pe, rows_copied, s + 1)
                if has(s, -2):
                    at_least(pe, result_taken, s - 1)
                if has(s, 1):
                    pe.wait_ge(nparts_ready, s + 2)
                if has(s, -1):
                    pe.wait_ge(av_copied, s)
                    for c in range(4):
                        ins = pe.matmul(M_AV[:, c, :, :].rearrange("p j i -> p (j i)"), avs[:, c * P:(c + 1) * P],
                                        pick[:, :, :].rearrange("p j i -> p (j i)"), start=True, stop=True)
                if has(s, 1):
                    ins = pe.transpose(M_NM, nparts[:, :, :, :].rearrange("p h a t -> p (h a t)"), identb[:, :])
                ins.then_inc(misc_ready, 1)

            def step(s, u, rnd):
                if has(s, 2):
                    w = (u + 2) % QBUF
                    pe.wait_ge(loads[w], (rnd + (u + 2) // QBUF) * 192 + 192)
                if has(s, 0):
                    pe.wait_ge(shifts_in[u], rnd * 32 + 32)
                for t in range(TB):
                    if has(s, 0):
                        keyed(s, u, t, 0)
                        keyed(s, u, t, 1)
                    if has(s, 2):
                        scores_turn(s, u, 2 * t)
                    if has(s, 0):
                        keyed(s, u, t, 2)
                    if t > 0 and has(s, 0):
                        values(s, u, t - 1)
                    elif t == 0 and has(s, -1):
                        values(s - 1, (u + 3) % QBUF, TB - 1)
                    if has(s, 0):
                        keyed(s, u, t, 3)
                    if has(s, 2):
                        scores_turn(s, u, 2 * t + 1)
                    if t == 2 and not (isinstance(s, int) and s < -1):
                        misc(s, u)
            steps(pe, step)


def phase_moe(nc, Wr, norm_w, Wg, Wu, Wd, f_norm, fWg, fWu, fWd, slots_in, slots_out, x, att, ident, identb, out):
    with ExitStack() as ctx:
        def sb(name, shape, dt):
            return ctx.enter_context(nc.sbuf_tensor(name, shape, dt))

        shared = att[:, :, :, :, :].rearrange("p a b c d -> p (a b c d)").rearrange("p (t d) -> p t d", d=D)
        norms = sb("norms", [P, E + 1], F32)
        weight = sb("weight", [P, NT, 2], F32)
        both = sb("both", [P, NT], F32)
        slot_of = sb("slot_of", [P, NT, 2], U32)
        route(nc, Wr, norm_w, f_norm, fWg, fWu, fWd, slots_in, x, att, shared, norms, weight, both, slot_of,
              ident)
        experts(nc, Wg, Wu, Wd, slots_in, slots_out, norms, ident)
        combine(nc, slots_out, x, shared, weight, both, slot_of, out)


def route(nc, Wr, norm_w, f_norm, fWg, fWu, fWd, slots_in, x, att, shared, norms, weight, both, slot_of, ident):
    with ExitStack() as ctx:
        def sb(name, shape, dt):
            return ctx.enter_context(nc.sbuf_tensor(name, shape, dt))

        def ps(name, shape, dt):
            return ctx.enter_context(nc.psum_tensor(name, shape, dt))

        def sem(name):
            return ctx.enter_context(nc.semaphore(name))

        norm_rows = sb("norm_rows", [E + 1, D], F32)
        fw_rows = sb("fw_rows", [P, 2 * F4], F32)
        rw = sb("rw", [P, RW], F32)
        fwd = sb("fwd", [F4, D], F32)
        before = sb("before", [P, P], BF16)
        ones = sb("ones", [P, P], BF16)
        iota_e = sb("iota_e", [P, E], F32)
        carry = sb("carry", [P, E], F32)
        power = sb("power2", [P, TB], F32)
        x2 = sb("x2", [P, TB, D], F32)
        x2T = sb("x2T", [P, S], F32)
        junk = sb("junk", [P, TB, D], F32)
        stats = sb("stats2", [P, TB, 6], F32)
        mv = sb("mv2", [P, TB, 2], F32)
        veps = sb("veps2", [P, TB], F32)
        rstd = sb("rstd2", [P, TB], F32)
        shift = sb("shift2", [P, TB], F32)
        ss = sb("ss", [P, TB], F32)
        meps = sb("meps", [P, TB], F32)
        rs = sb("rs", [P, TB], F32)
        logits = sb("logits", [P, TB, E], F32)
        ranked = sb("ranked", [P, TB, E], F32)
        index = sb("index", [P, TB, E], U32)
        chosen = sb("chosen", [P, TB, 2], F32)
        expo = sb("expo", [P, TB, E], F32)
        total = sb("total", [P, TB], F32)
        inv = sb("inv", [P, TB], F32)
        onehot = sb("onehot", [P, 2, TB, E], F32)
        given = sb("given", [P, TB, E], BF16)
        gpos = sb("gpos", [P, TB, E], F32)
        mpos = sb("mpos", [P, 2, TB, E], F32)
        pos = sb("pos", [P, TB, 2], F32)
        keep = sb("keep", [P, TB, 2], F32)
        cpos = sb("cpos", [P, TB, 2], F32)
        far = sb("far", [P, TB, 2], F32)
        send = sb("send", [P, TB, 2], F32)
        send_to = sb("send_to", [P, TB, 2], U32)
        gu = sb("gu", [P, TB, 2 * F4], F32)
        gelu = sb("gelu", [P, TB, F4], F32)
        act_out = sb("act_out", [P, TB, F4], F32)
        guT = sb("guT", [F4, S], F32)

        ps_r = ps("ps_r", [P, TB, 256], F32)
        ps_pos = ps("ps_pos", [P, HALF], F32)
        ps_T = ps("ps_T2", [P, TB, P], F32)

        w_in = sem("w_in2")
        pool_set = sem("pool_set")
        norms_ps = sem("norms_ps")
        rw_ready = sem("rw_ready")
        x1_ready = sem("x1_ready")
        stats_ready = sem("stats_ready2")
        var_ready = sem("var_ready2")
        rstd_ready = sem("rstd_ready2")
        shift_ready = sem("shift_ready2")
        x2_ready = sem("x2_ready")
        ss_ready = sem("ss_ready")
        meps_ready = sem("meps_ready")
        rs_ready = sem("rs_ready")
        base_ready = sem("base_ready")
        turned = sem("turned")
        x2T_ready = sem("x2T_ready")
        routed = sem("routed")
        gu_ready = sem("gu_ready")
        gelu_ready = sem("gelu_ready")
        act_ready = sem("act_ready")
        guT_ready = sem("guT_ready")
        shared_ready = sem("shared_ready")
        diff_ready = sem("diff_ready")
        expo_ready = sem("expo_ready")
        given_ready = sem("given_ready")
        pos_ps = sem("pos_ps")
        pos_taken = sem("pos_taken")
        send_ready = sem("send_ready")
        sent = sem("sent")
        passed = sem("passed2")
        dve_own = sem("dve_own2")
        act_own = sem("act_own2")

        block = ctx.enter_context(nc.Block())

        @block.sync
        def _(sp):
            sp.dma_start(norm_rows[0:E, :], norm_w).then_inc(w_in, 16)
            sp.dma_start(norm_rows[E:E + 1, :], f_norm.rearrange("(a d) -> a d", a=1)).then_inc(w_in, 16)
            sp.dma_start(rw[:, 0:E], Wr).then_inc(w_in, 16)
            sp.dma_start(fw_rows[:, 0:F4], fWg).then_inc(w_in, 16)
            sp.dma_start(fw_rows[:, F4:2 * F4], fWu).then_inc(w_in, 16)
            sp.dma_start(fwd[:, :], fWd).then_inc(w_in, 16)

        @block.gpsimd
        def _(pool):
            pool.memset(power[:, :], -0.5).then_inc(pool_set, 1)
            pool.memset(ones[:, :], 1.0).then_inc(pool_set, 1)
            pool.iota(iota_e[:, :], pattern=[[1, E]], base=0, channel_multiplier=0,
                      allow_small_or_imprecise_dtypes=True).then_inc(pool_set, 1)
            pool.wait_ge(pool_set, 3)
            pool.affine_select(out=before[:, :], in_=ones[:, :], compare_op=ALU.is_gt, fill=0.0, base=0,
                               pattern=[[1, P]], channel_multiplier=-1).then_inc(pool_set, 1)
            att_rows = att[:, :, :, :, :].rearrange("p m h t d -> p t (m h) d")
            x_rows = x[:, :, :].rearrange("p t (m d) -> p t m d", d=DH)
            with pool.Fori(0, B) as b:
                xb = x_rows[:, bass.ds(b * TB, TB), :, :]
                pool.tensor_tensor(xb, xb, att_rows[:, :, bass.ds(b * H, H), :], ALU.add).then_inc(x1_ready, 1)
                pool.wait_ge(var_ready, b + 1)
                pool.tensor_tensor(rstd[:, :], veps[:, :], power[:, :], ALU.pow).then_inc(rstd_ready, 1)
                pool.wait_ge(meps_ready, b + 1)
                pool.tensor_tensor(rs[:, :], meps[:, :], power[:, :], ALU.pow).then_inc(rs_ready, 1)
                wait_apart(pool, x2_ready, b + 1, passed)
                xf = x[:, bass.ds(b * TB, TB), :]
                pool.tensor_tensor(xf, xf, x2[:, :, :], ALU.add).then_inc(base_ready, 1)
                wait_apart(pool, send_ready, b + 1, passed)
                for t in range(TB):
                    for k in range(2):
                        pool.indirect_dma_start(
                            slots_in, bass.IndirectOffsetOnAxis(ap=send_to[:, t, k:k + 1], axis=0), x2[:, t, :], None,
                            bounds_check=E * CAP - 1, oob_is_err=False).then_inc(sent, 16)
            pool.wait_ge(sent, B * TB * 2 * 16)

        @block.scalar
        def _(act):
            own = Chain(act, act_own)
            with act.Fori(0, B) as b:
                own.loop(b, 1)
                act.wait_ge(shift_ready, b + 1)
                act.wait_ge(sent, b * (TB * 2 * 16))
                act.wait_ge(base_ready, b)
                act.wait_ge(turned, b * 2)
                for t in range(TB):
                    ins = act.activation(x2[:, t, :], x[:, bass.ds(b * TB + t, 1), :], ACT.Identity,
                                         bias=shift[:, t:t + 1], scale=rstd[:, t:t + 1])
                own(ins)
                act.sem_inc(x2_ready, 1)
                for t in range(TB):
                    ins = act.activation(junk[:, t, :], x2[:, t, :], ACT.Square, accum_out=ss[:, t:t + 1])
                ins.then_inc(ss_ready, 1)
                act.wait_ge(turned, b * 2 + 1)
                act.activation(x2T[:, :], ps_T[:, :, :], ACT.Copy).then_inc(x2T_ready, 1)
                act.wait_ge(diff_ready, b + 1)
                act.activation(expo[:, :, :], expo[:, :, :], ACT.Exp).then_inc(expo_ready, 1)
                act.wait_ge(gu_ready, b + 1)
                act.activation(gelu[:, :, :], gu[:, :, 0:F4], ACT.Gelu).then_inc(gelu_ready, 1)
                act.wait_ge(turned, b * 2 + 2)
                act.activation(guT[:, :], ps_T[0:F4, :, :], ACT.Copy).then_inc(guT_ready, 1)
                act.wait_ge(shared_ready, b * 2 + 1)
                act.activation(shared[:, bass.ds(b * TB, TB), :], ps_T[:, :, :], ACT.Copy).then_inc(shared_ready, 1)
            own.end(B)

        @block.vector
        def _(dve):
            own = Chain(dve, dve_own)
            own(dve.memset(carry[:, :], 0.0))
            dve.wait_ge(norms_ps, 1)
            own(dve.tensor_copy(norms[:, :], ps_pos[:, 0:E + 1]))
            dve.wait_ge(w_in, 6 * 16)
            dve.tensor_scalar(rw[:, E:RW], fw_rows[:, :], norms[:, E:E + 1], None, ALU.mult).then_inc(rw_ready, 1)
            dve.wait_ge(pool_set, 3)
            own.k, own.base = 0, 2
            with dve.Fori(0, B) as b:
                own.loop(b, 21)
                dve.wait_ge(x1_ready, b + 1)
                for t in range(TB):
                    ins = dve.bn_stats(stats[:, t, :], x[:, bass.ds(b * TB + t, 1), :])
                own(ins)
                dve.sem_inc(stats_ready, 1)
                for t in range(TB):
                    ins = dve.bn_aggr(mv[:, t, :], stats[:, t, :])
                own(ins)
                dve.tensor_scalar(veps[:, :], mv[:, :, 1], LN_EPS, None, ALU.add).then_inc(var_ready, 1)
                dve.wait_ge(rstd_ready, b + 1)
                dve.scalar_tensor_tensor(out=shift[:, :], in0=mv[:, :, 0], scalar=-1.0, in1=rstd[:, :],
                                         op0=ALU.mult, op1=ALU.mult).then_inc(shift_ready, 1)
                dve.wait_ge(ss_ready, b + 1)
                dve.tensor_scalar(meps[:, :], ss[:, :], 1.0 / D, RMS_EPS, ALU.mult, ALU.add).then_inc(meps_ready, 1)
                dve.wait_ge(routed, b + 1)
                own(dve.tensor_copy(logits[:, :, :], ps_r[:, :, 0:E]))
                dve.wait_ge(rs_ready, b + 1)
                dve.tensor_tensor(gu[:, :, :], ps_r[:, :, E:RW], rs[:, :].rearrange("p (t a) -> p t a", a=1)
                                  .broadcast_to((P, TB, 2 * F4)), ALU.mult).then_inc(gu_ready, 1)
                for t in range(TB):
                    ins = dve.max(ranked[:, t, :], logits[:, t, :])
                own(ins)
                own(dve.tensor_tensor(expo[:, :, :], ranked[:, :, :], ranked[:, :, 0:1].broadcast_to((P, TB, E)),
                                      ALU.subtract))
                dve.sem_inc(diff_ready, 1)
                for t in range(TB):
                    ins = dve.max_index(index[:, t, :], ranked[:, t, :], logits[:, t, :])
                own(ins)
                own(dve.tensor_copy(chosen[:, :, :], index[:, :, 0:2]))
                for k in range(2):
                    ins = dve.tensor_tensor(
                        onehot[:, k, :, :], iota_e[:, :].rearrange("p (a e) -> p a e", a=1).broadcast_to((P, TB, E)),
                        chosen[:, :, k:k + 1].broadcast_to((P, TB, E)), ALU.is_equal)
                own(ins)
                dve.tensor_tensor(given[:, :, :], onehot[:, 0, :, :], onehot[:, 1, :, :], ALU.add).then_inc(given_ready, 1)
                dve.wait_ge(expo_ready, b + 1)
                own(dve.tensor_reduce(total[:, :], expo[:, :, :], AX.X, ALU.add))
                own(dve.reciprocal(inv[:, :], total[:, :]))
                dve.tensor_tensor(weight[:, bass.ds(b * TB, TB), :], expo[:, :, 0:2],
                                  inv[:, :].rearrange("p (t a) -> p t a", a=1).broadcast_to((P, TB, 2)), ALU.mult)
                dve.wait_ge(pos_ps, b + 1)
                own(dve.tensor_tensor(gpos[:, :, :], ps_pos[:, 0:TB * E].rearrange("p (t e) -> p t e", e=E),
                                      carry[:, :].rearrange("p (a e) -> p a e", a=1).broadcast_to((P, TB, E)),
                                      ALU.add))
                own(dve.tensor_tensor(carry[:, :], ps_pos[:, TB * E:(TB + 1) * E], carry[:, :], ALU.add))
                dve.sem_inc(pos_taken, 1)
                for k in range(2):
                    ins = dve.tensor_tensor(mpos[:, k, :, :], gpos[:, :, :], onehot[:, k, :, :], ALU.mult)
                own(ins)
                own(dve.tensor_reduce(pos[:, :, :].rearrange("p t k -> p k t"), mpos[:, :, :, :], AX.X, ALU.add))
                own(dve.tensor_scalar(keep[:, :, :], pos[:, :, :], float(CAP), None, ALU.is_lt))
                own(dve.tensor_scalar(cpos[:, :, :], pos[:, :, :], float(CAP - 1), None, ALU.min))
                own(dve.scalar_tensor_tensor(out=slot_of[:, bass.ds(b * TB, TB), :], in0=chosen[:, :, :],
                                             scalar=float(CAP), in1=cpos[:, :, :], op0=ALU.mult, op1=ALU.add))
                own(dve.tensor_scalar(far[:, :, :], keep[:, :, :], -float(FAR), float(FAR), ALU.mult, ALU.add))
                own(dve.scalar_tensor_tensor(out=send[:, :, :], in0=chosen[:, :, :], scalar=float(CAP),
                                             in1=pos[:, :, :], op0=ALU.mult, op1=ALU.add))
                dve.wait_ge(sent, b * (TB * 2 * 16))
                dve.tensor_tensor(send_to[:, :, :], send[:, :, :], far[:, :, :], ALU.add).then_inc(send_ready, 1)
                own(dve.tensor_tensor(both[:, bass.ds(b * TB, TB)], keep[:, :, 0], keep[:, :, 1], ALU.mult))
                dve.wait_ge(gelu_ready, b + 1)
                dve.tensor_tensor(act_out[:, :, :], gelu[:, :, :], gu[:, :, F4:2 * F4], ALU.mult).then_inc(act_ready, 1)
                own(dve.tensor_copy(total[:, :], total[:, :]))
            own.end(B)

        @block.tensor
        def _(pe):
            pe.wait_ge(w_in, 6 * 16)
            pe.transpose(ps_pos[:, 0:E + 1], norm_rows[:, :], ident[0:E + 1, 0:E + 1]).then_inc(norms_ps, 1)
            pe.wait_ge(rw_ready, 1)
            pe.wait_ge(pool_set, 4)
            with pe.Fori(0, B) as b:
                pe.wait_ge(x2_ready, b + 1)
                pe.wait_ge(shared_ready, b * 2)
                for t in range(TB):
                    ins = pe.transpose(ps_T[:, t, :], x2[:, t, :], ident[:, :])
                ins.then_inc(turned, 1)
                pe.wait_ge(x2T_ready, b + 1)
                pe.wait_ge(gu_ready, b)
                for t in range(TB):
                    ins = pe.matmul(ps_r[:, t, 0:RW], x2T[:, t * P:(t + 1) * P], rw[:, :], start=True, stop=True)
                ins.then_inc(routed, 1)
                pe.wait_ge(given_ready, b + 1)
                pe.wait_ge(pos_taken, b)
                pe.matmul(ps_pos[:, 0:TB * E], before[:, :], given[:, :, :], start=True, stop=False,
                          skip_group_check=True)
                for j in range(TB):
                    ins = pe.matmul(ps_pos[:, (j + 1) * E:(TB + 1) * E].rearrange("p (t e) -> p t e", e=E), ones[:, :],
                                    given[:, j:j + 1, :].broadcast_to((P, TB - j, E)), start=False,
                                    stop=(j == TB - 1), skip_group_check=True)
                ins.then_inc(pos_ps, 1)
                wait_apart(pe, act_ready, b + 1, passed)
                for t in range(TB):
                    ins = pe.transpose(ps_T[0:F4, t, :], act_out[:, t, :], ident[:, :])
                ins.then_inc(turned, 1)
                pe.wait_ge(guT_ready, b + 1)
                for t in range(TB):
                    ins = pe.matmul(ps_T[:, t, :], guT[:, t * P:(t + 1) * P], fwd[:, :], start=True, stop=True)
                ins.then_inc(shared_ready, 1)


def experts(nc, Wg, Wu, Wd, slots_in, slots_out, norms, ident):
    with ExitStack() as ctx:
        def sb(name, shape, dt):
            return ctx.enter_context(nc.sbuf_tensor(name, shape, dt))

        def ps(name, shape, dt):
            return ctx.enter_context(nc.psum_tensor(name, shape, dt))

        def sem(name):
            return ctx.enter_context(nc.semaphore(name))

        NB = 2
        wg = [sb(f"wg{w}", [P, F], F32) for w in range(NB)]
        wu = [sb(f"wu{w}", [P, F], F32) for w in range(NB)]
        wd = [sb(f"wd{w}", [P, FT, D], F32) for w in range(NB)]
        rows = [sb(f"rows{w}", [P, CT, D], F32) for w in range(NB)]
        yrows = [sb(f"yrows{w}", [P, CT, D], F32) for w in range(NB)]
        junk = sb("junk2", [P, CT, D], F32)
        ss = sb("ss2", [P, CT], F32)
        meps = sb("meps2", [P, CT], F32)
        rs = sb("rs2", [P, CT], F32)
        power = sb("power3", [P, CT], F32)
        h = sb("h", [P, CT, D], F32)
        hT = sb("hT", [P, CAP], F32)
        gelu = sb("gelu2", [P, FT, CAP], F32)
        gu = sb("gu2", [P, FT, CAP], F32)
        ps_h = ps("ps_h", [P, CAP], F32)
        ps_g = ps("ps_g", [P, FT, CAP], F32)
        ps_u = ps("ps_u", [P, FT, CAP], F32)
        ps_y = ps("ps_y", [P, CT, D], F32)

        w_in = [sem(f"e_w_in{w}") for w in range(NB)]
        rows_in = [sem(f"e_rows_in{w}") for w in range(NB)]
        stored = [sem(f"e_stored{w}") for w in range(NB)]
        power_set = sem("e_power_set")
        ss_ready = sem("e_ss_ready")
        meps_ready = sem("e_meps_ready")
        rs_ready = sem("e_rs_ready")
        h_ready = sem("e_h_ready")
        turned = sem("e_turned")
        hT_ready = sem("e_hT_ready")
        gate_ps = sem("e_gate_ps")
        up_ps = sem("e_up_ps")
        gelu_ready = sem("e_gelu_ready")
        gu_ready = sem("e_gu_ready")
        down_ps = sem("e_down_ps")
        y_ready = sem("e_y_ready")

        block = ctx.enter_context(nc.Block())

        def each(eng, step):
            for e in range(NB):
                step(e, e, 0)
            with eng.Fori(1, E // NB) as i:
                for w in range(NB):
                    step(i * NB + w, w, i)

        @block.sync
        def _(sp):
            def step(e, w, rnd):
                if not isinstance(e, int):
                    sp.wait_ge(down_ps, e - 1)
                    sp.wait_ge(y_ready, e - 1)
                sp.dma_start(wg[w][:, :], Wg[bass.ds(e, 1), :, :].rearrange("a h f -> h (a f)")).then_inc(w_in[w], 16)
                sp.dma_start(wu[w][:, :], Wu[bass.ds(e, 1), :, :].rearrange("a h f -> h (a f)")).then_inc(w_in[w], 16)
                sp.dma_start(wd[w][:, :, :], Wd[bass.ds(e, 1), :, :].rearrange("a (t p) h -> p (a t) h", p=P)).then_inc(w_in[w], 16)
                sp.dma_start(rows[w][:, :, :], slots_in[bass.ds(e * CAP, CAP), :].rearrange("(t p) h -> p t h", p=P)).then_inc(rows_in[w], 16)
            each(sp, step)

        @block.gpsimd
        def _(pool):
            pool.memset(power[:, :], -0.5).then_inc(power_set, 1)
            pool.wait_ge(power_set, 1)

            def step(e, w, rnd):
                pool.wait_ge(meps_ready, e + 1)
                pool.tensor_tensor(rs[:, :], meps[:, :], power[:, :], ALU.pow).then_inc(rs_ready, 1)
                pool.wait_ge(y_ready, e + 1)
                pool.dma_start(slots_out[bass.ds(e * CAP, CAP), :].rearrange("(t p) h -> p t h", p=P), yrows[w][:, :, :]).then_inc(stored[w], 16)
            each(pool, step)
            for w in range(NB):
                pool.wait_ge(stored[w], E // NB * 16)

        @block.scalar
        def _(act):
            def step(e, w, rnd):
                act.wait_ge(rows_in[w], rnd * 16 + 16)
                if not isinstance(e, int) or e > 0:
                    act.wait_ge(meps_ready, e)
                for t in range(CT):
                    ins = act.activation(junk[:, t, :], rows[w][:, t, :], ACT.Square, accum_out=ss[:, t:t + 1])
                ins.then_inc(ss_ready, 1)
                act.wait_ge(rs_ready, e + 1)
                for t in range(CT):
                    ins = act.activation(h[:, t, :], rows[w][:, t, :], ACT.Copy, scale=rs[:, t:t + 1])
                ins.then_inc(h_ready, 1)
                act.wait_ge(turned, e + 1)
                act.activation(hT[:, :], ps_h[:, :], ACT.Copy, scale=norms[:, bass.ds(e, 1)]).then_inc(hT_ready, 1)
                act.wait_ge(gate_ps, e + 1)
                act.activation(gelu[:, :, :], ps_g[:, :, :], ACT.Gelu).then_inc(gelu_ready, 1)
            each(act, step)

        @block.vector
        def _(dve):
            def step(e, w, rnd):
                dve.wait_ge(ss_ready, e + 1)
                dve.tensor_scalar(meps[:, :], ss[:, :], 1.0 / D, RMS_EPS, ALU.mult, ALU.add).then_inc(meps_ready, 1)
                dve.wait_ge(gelu_ready, e + 1)
                dve.wait_ge(up_ps, e + 1)
                dve.tensor_tensor(gu[:, :, :], gelu[:, :, :], ps_u[:, :, :], ALU.mult).then_inc(gu_ready, 1)
                dve.wait_ge(down_ps, e + 1)
                if not isinstance(e, int):
                    dve.wait_ge(stored[w], rnd * 16)
                dve.tensor_tensor(yrows[w][:, :, :], ps_y[:, :, :], rows[w][:, :, :], ALU.add).then_inc(y_ready, 1)
            each(dve, step)

        @block.tensor
        def _(pe):
            def step(e, w, rnd):
                pe.wait_ge(h_ready, e + 1)
                for t in range(CT):
                    ins = pe.transpose(ps_h[:, t * P:(t + 1) * P], h[:, t, :], ident[:, :])
                ins.then_inc(turned, 1)
                pe.wait_ge(hT_ready, e + 1)
                pe.wait_ge(w_in[w], rnd * 48 + 48)
                for f in range(FT):
                    ins = pe.matmul(ps_g[:, f, :], wg[w][:, f * P:(f + 1) * P], hT[:, :], start=True, stop=True)
                ins.then_inc(gate_ps, 1)
                for f in range(FT):
                    ins = pe.matmul(ps_u[:, f, :], wu[w][:, f * P:(f + 1) * P], hT[:, :], start=True, stop=True)
                ins.then_inc(up_ps, 1)
                pe.wait_ge(gu_ready, e + 1)
                if not isinstance(e, int) or e > 0:
                    pe.wait_ge(y_ready, e)
                for t in range(CT):
                    for f in range(FT):
                        ins = pe.matmul(ps_y[:, t, :], gu[:, f, t * P:(t + 1) * P], wd[w][:, f, :],
                                        start=(f == 0), stop=(f == FT - 1))
                ins.then_inc(down_ps, 1)
            each(pe, step)


def combine(nc, slots_out, x, shared, weight, both, slot_of, out):
    with ExitStack() as ctx:
        def sb(name, shape, dt):
            return ctx.enter_context(nc.sbuf_tensor(name, shape, dt))

        def sem(name):
            return ctx.enter_context(nc.semaphore(name))

        NB = 2
        slots = [sb(f"slots{w}", [P, TB, 2], U32) for w in range(NB)]
        got = [sb(f"got{w}", [P, TB, 2, D], F32) for w in range(NB)]
        mixed = sb("mixed", [P, 2, TB, D], F32)
        slots_set = sem("slots_set")
        gathered = [sem(f"gathered{w}") for w in range(NB)]
        used = sem("used")
        own_sem = sem("dve_own3")
        rows_ready = sem("rows_ready")
        written = sem("written")

        block = ctx.enter_context(nc.Block())

        def each(eng, step):
            for b in range(NB):
                step(b, b, 0)
            with eng.Fori(1, B // NB) as i:
                for w in range(NB):
                    step(i * NB + w, w, i)

        @block.gpsimd
        def _(pool):
            def step(b, w, rnd):
                if not isinstance(rnd, int) or rnd > 0:
                    pool.wait_ge(gathered[w], rnd * (TB * 2 * 16))
                    pool.wait_ge(used, b - 1)
                pool.tensor_copy(slots[w][:, :, :], slot_of[:, bass.ds(b * TB, TB), :]).then_inc(slots_set, 1)
                pool.wait_ge(slots_set, b + 1)
                for t in range(TB):
                    for k in range(2):
                        pool.indirect_dma_start(got[w][:, t, k, :], None, slots_out,
                                                bass.IndirectOffsetOnAxis(ap=slots[w][:, t, k:k + 1], axis=0),
                                                bounds_check=E * CAP - 1, oob_is_err=False).then_inc(gathered[w], 16)
            each(pool, step)

        @block.vector
        def _(dve):
            own = Chain(dve, own_sem)

            def step(b, w, rnd):
                at = bass.ds(b * TB, TB)
                dve.wait_ge(gathered[w], rnd * (TB * 2 * 16) + TB * 2 * 16)
                for k in range(2):
                    ins = dve.tensor_tensor(mixed[:, k, :, :], got[w][:, :, k, :],
                                            weight[:, at, k:k + 1].broadcast_to((P, TB, D)), ALU.mult)
                ins.then_inc(used, 1)
                dve.wait_ge(used, b + 1)
                dve.tensor_tensor(mixed[:, 0, :, :], mixed[:, 0, :, :], mixed[:, 1, :, :], ALU.add).then_inc(own_sem, 1)
                dve.wait_ge(own_sem, b * 2 + 1)
                dve.copy_predicated(shared[:, at, :], both[:, at].bitcast(U32).rearrange("p (t a) -> p t a", a=1)
                                    .broadcast_to((P, TB, D)), mixed[:, 0, :, :]).then_inc(own_sem, 1)
                dve.wait_ge(own_sem, b * 2 + 2)
                dve.tensor_tensor(x[:, at, :], x[:, at, :], shared[:, at, :], ALU.add).then_inc(rows_ready, 1)
            each(dve, step)

        @block.sync
        def _(sp):
            for b in range(B):
                sp.wait_ge(rows_ready, b + 1)
                sp.dma_start(out[b].rearrange("(t p) d -> p t d", p=P), x[:, b * TB:(b + 1) * TB, :]).then_inc(written, 16)
            sp.wait_ge(written, B * 16)


_INS = ['L0_attn_z', 'L0_attn_W_qkv', 'L0_ffn_Wr', 'L0_ffn_norm_w', 'L0_ffn_Wg', 'L0_ffn_Wu', 'L0_ffn_Wd',
        'L0_ffn_f_norm', 'L0_ffn_fWg', 'L0_ffn_fWu', 'L0_ffn_fWd']
_OUTS = [((B, S, D), 'float32')]


def kernel(**inputs):
    import numpy as _np
    import concourse.bacc as _bacc
    from concourse import mybir as _mybir
    from concourse.bass_utils import run_bass_kernel_spmd as _run

    nc = _bacc.Bacc("TRN2", target_bir_lowering=False, num_devices=1)
    arrays, args = {}, []
    for name in _INS:
        a = _np.ascontiguousarray(inputs[name])
        arrays[f"in_{name}_dram"] = a
        args.append(nc.dram_tensor(f"in_{name}_dram", a.shape, _mybir.dt.from_np(a.dtype), kind="ExternalInput").ap())
    for i, (shape, dtype) in enumerate(_OUTS):
        dt = _mybir.dt.from_np(_np.dtype(dtype))
        args.append(nc.dram_tensor(f"out_{i}_dram", shape, dt, kind="ExternalOutput").ap())
    attention_moe(nc, *args)
    r = _run(nc, [arrays], core_ids=[0])
    return r.results[0]["out_0_dram"]
```

```python
from contextlib import ExitStack

import concourse.bass as bass
from concourse import mybir

F32 = mybir.dt.float32
BF16 = mybir.dt.bfloat16
U32 = mybir.dt.uint32
ALU = mybir.AluOpType
ACT = mybir.ActivationFunctionType
AX = mybir.AxisListType

P = 128
B, S, D = 4, 1024, 128
N = B * S
H, DH = 16, 8
NPAIR = B * H // 2
TB = S // P
NT = N // P
HALF = 512
NPART = 3
PROD = NPART * NPART * DH
SHIFT = 96
KROWS = SHIFT + NPART
QBUF = 4
PRING = 4
E = 8
CAP = 512
assert E * CAP == NPAIR * P and N == NPAIR * P
CT = CAP // P
F = 256
FT = F // P
F4 = 64
ROW = D + 2
RW = E + 2 * F4
LN_EPS = 1e-5
RMS_EPS = 1e-6
SOFTMAX_SCALE = float(DH) ** -0.5
FAR = 1 << 16


def wait_apart(eng, semaphore, value, passed):
    eng.wait_ge(semaphore, value)
    eng.sem_inc(passed, 1)


class Chain:

    def __init__(self, eng, sem):
        self.eng, self.sem, self.base, self.k, self.it, self.per = eng, sem, 0, 0, None, 0

    def loop(self, it, per):
        self.it, self.per, self.k = it, per, 0

    def end(self, times):
        assert self.k == self.per, self.k
        self.base += times * self.per
        self.it, self.k = None, 0

    def __call__(self, ins):
        self.k += 1
        ins.then_inc(self.sem, 1)
        if self.it is None:
            self.eng.wait_ge(self.sem, self.base + self.k)
        else:
            self.eng.wait_ge(self.sem, self.it * self.per + (self.base + self.k))


def run_steps(eng, step, start, first, last, stop, unroll):
    for s in range(start, first):
        step(s, s % unroll, s // unroll)
    assert (last - first + 1) % unroll == 0
    with eng.Fori(0, (last - first + 1) // unroll) as i:
        for u in range(unroll):
            step(i * unroll + (first + u), (first + u) % unroll, i + (first + u) // unroll)
    for s in range(last + 1, stop):
        step(s, s % unroll, s // unroll)


def has_item(s, offset, n):
    return not isinstance(s, int) or 0 <= s + offset < n


def at_least(eng, semaphore, value):
    if not isinstance(value, int) or value > 0:
        eng.wait_ge(semaphore, value)


def attention_moe(nc, z, W_qkv, Wr, norm_w, Wg, Wu, Wd, f_norm, fWg, fWu, fWd, out, debug=None):
    with ExitStack() as ctx:
        def sb(name, shape, dt):
            return ctx.enter_context(nc.sbuf_tensor(name, shape, dt))

        q_parts = nc.dram_tensor("q_parts", (NPART, NPAIR * 2 * DH, S), BF16, kind="Internal").ap()
        k_parts = nc.dram_tensor("k_parts", (NPART, NPAIR * 2 * DH, S), BF16, kind="Internal").ap()
        slots_in = nc.dram_tensor("slots_in", (E * CAP, ROW), F32, kind="Internal").ap()
        tok_out = nc.dram_tensor("tok_out", (N * 2, D), F32, kind="Internal").ap()

        x = sb("x", [P, NT, D], F32)
        ident = sb("ident", [P, P], F32)
        identb = sb("identb", [P, P], BF16)
        qo = [sb(f"qo{u}", [P, 2, S], BF16) for u in range(QBUF)]
        ko = [sb(f"ko{u}", [P, 2, S], BF16) for u in range(QBUF)]
        v_all = sb("v_all", [P, NPAIR, TB, 2, DH + 1], F32)
        gu_all = sb("gu_all", [P, NT, 2 * F4], F32)
        overflow = sb("overflow", [P, NT], F32)
        norms = sb("norms", [P, E + 1], F32)

        phase_qkv(nc, z, W_qkv, q_parts, k_parts, x, v_all, qo, ko, ident, identb)
        phase_attention(nc, q_parts, k_parts, Wr, norm_w, f_norm, fWg, fWu, slots_in, tok_out, v_all, qo, ko,
                        x, gu_all, overflow, norms, ident, identb)
        phase_experts(nc, Wg, Wu, Wd, fWd, slots_in, tok_out, x, gu_all, overflow, norms, ident)
        phase_combine(nc, tok_out, x, out)


def phase_qkv(nc, z, W_qkv, q_parts, k_parts, x, v_all, qo, ko, ident, identb):
    GT = 4
    G = NT // GT
    GC = GT * P
    assert GC == HALF
    with ExitStack() as ctx:
        def sb(name, shape, dt):
            return ctx.enter_context(nc.sbuf_tensor(name, shape, dt))

        def ps(name, shape, dt):
            return ctx.enter_context(nc.psum_tensor(name, shape, dt))

        def sem(name):
            return ctx.enter_context(nc.semaphore(name))

        w_rows = sb("w_rows", [P, 3, D], F32)
        wT = sb("wT", [P, 3, H, DH], F32)
        zn = sb("zn", [P, 2, GT, D], F32)
        zT = sb("zT", [P, 2, GC], F32)
        stats = sb("stats", [P, 2, GT, 6], F32)
        mv = sb("mv", [P, 2, GT, 2], F32)
        veps = sb("veps", [P, 2, GT], F32)
        power = sb("power", [P, GT], F32)
        rstd = sb("rstd", [P, 2, GT], F32)
        part = sb("part", [P, 2, 2, NPART, GC], BF16)
        rest = sb("rest", [P, 2, GC], F32)

        ps_T = ps("ps_T", [P, 2, GC], F32)
        ps_qk = ps("ps_qk", [P, 2, 2, GC], F32)
        ps_v = ps("ps_v", [P, 2, GT, H // 2, 2, DH], F32)

        x_in = [sem(f"x_in{b}") for b in range(B)]
        w_in = sem("w_in")
        masks = sem("masks")
        ones_set = sem("ones_set")
        wT_ps = sem("wT_ps")
        wT_ready = sem("wT_ready")
        stats_done = sem("stats_done")
        mv_ready = sem("mv_ready")
        veps_ready = sem("veps_ready")
        rstd_ready = sem("rstd_ready")
        zn_ready = sem("zn_ready")
        zT_ps = sem("zT_ps")
        zT_ready = sem("zT_ready")
        qk_ps = sem("qk_ps")
        v_ps = sem("v_ps")
        hi_ready = sem("hi_ready")
        rest_ready = sem("rest_ready")
        mid_ready = sem("mid_ready")
        lo_ready = sem("lo_ready")
        v_ready = sem("v_ready")
        parts_out = [sem(f"parts_out{w}") for w in range(2)]
        passed = sem("passed0")

        block = ctx.enter_context(nc.Block())

        def steps(eng, step):
            run_steps(eng, step, 0, 4, G - 1, G + 2, 2)

        def has(s, offset):
            return has_item(s, offset, G)

        @block.sync
        def _(sp):
            for b in range(B):
                if b == 1:
                    sp.dma_start(w_rows[:, :, :], W_qkv.rearrange("(c p) d -> p c d", p=P)).then_inc(w_in, 16)
                sp.dma_start(x[:, b * TB:(b + 1) * TB, :], z[b].rearrange("(t p) d -> p t d", p=P)).then_inc(x_in[b], 16)

            def step(s, w, rnd):
                if has(s, -2):
                    for qk, store in enumerate((q_parts, k_parts)):
                        sp.wait_ge(lo_ready, s * 2 + (qk - 3))
                        for i in range(NPART):
                            sp.dma_start(store[i, bass.ds((rnd - 1) * P, P), w * GC:(w + 1) * GC],
                                         part[:, w, qk, i, :]).then_inc(parts_out[w], 16)
            steps(sp, step)
            for w in range(2):
                sp.wait_ge(parts_out[w], (G // 2) * 2 * NPART * 16)

        @block.gpsimd
        def _(pool):
            pool.memset(ident[:, :], 0.0).then_inc(masks, 1)
            pool.memset(identb[:, :], 0.0).then_inc(masks, 1)
            pool.wait_ge(masks, 2)
            for m in (ident, identb):
                pool.affine_select(out=m[:, :], in_=m[:, :], compare_op=ALU.not_equal, fill=1.0, base=0,
                                   pattern=[[-1, P]], channel_multiplier=1).then_inc(masks, 1)
            pool.memset(power[:, :], -0.5).then_inc(masks, 1)
            pool.wait_ge(masks, 5)
            for u in range(QBUF):
                pool.memset(qo[u][64:P, :, :], 0.0).then_inc(ones_set, 1)
            pool.wait_ge(ones_set, QBUF)
            for u in range(QBUF):
                pool.memset(ko[u][64:SHIFT, :, :], 0.0).then_inc(ones_set, 1)
            pool.wait_ge(ones_set, 2 * QBUF)
            for u in range(QBUF):
                pool.memset(ko[u][SHIFT:P, :, :], 1.0).then_inc(ones_set, 1)
            pool.wait_ge(ones_set, 3 * QBUF)

            def step(s, w, rnd):
                if has(s, 0):
                    pool.wait_ge(veps_ready, s + 1)
                    pool.tensor_tensor(rstd[:, w, :], veps[:, w, :], power[:, :], ALU.pow).then_inc(rstd_ready, 1)
                if isinstance(s, int) and s == 1:
                    pool.memset(v_all[:, :, :, :, DH:DH + 1], 1.0).then_inc(ones_set, 1)
            steps(pool, step)

        @block.scalar
        def _(act):
            def step(s, w, rnd):
                v = 1 - w
                if has(s, -1):
                    act.wait_ge(zT_ps, s)
                    act.activation(zT[:, v, :], ps_T[:, v, :], ACT.Copy).then_inc(zT_ready, 1)
                if has(s, -2):
                    for qk in range(2):
                        act.wait_ge(qk_ps, s * 2 + (qk - 3))
                        if not isinstance(s, int) or s >= 4:
                            act.wait_ge(parts_out[w], rnd * (2 * NPART * 16) - (2 * NPART * 16))
                        act.activation(part[:, w, qk, 0, :], ps_qk[:, w, qk, :], ACT.Copy).then_inc(hi_ready, 1)
                    act.wait_ge(v_ps, s - 1)
                    for t in range(GT):
                        ins = act.activation(v_all[:, bass.ds((rnd - 1) * (H // 2), H // 2), w * GT + t, :, 0:DH],
                                             ps_v[:, w, t, :, :, :], ACT.Copy)
                    ins.then_inc(v_ready, 1)
                    for qk in range(2):
                        act.wait_ge(rest_ready, s * 2 + (qk - 3))
                        act.activation(part[:, w, qk, 1, :], rest[:, qk, :], ACT.Copy).then_inc(mid_ready, 1)
            steps(act, step)

        @block.vector
        def _(dve):
            dve.wait_ge(wT_ps, 1)
            for c in range(3):
                ins = dve.tensor_copy(wT[:, c, :, :], ps_qk[:, 0, 0, 0:3 * P].rearrange(
                    "p (h c d) -> p c h d", c=3, d=DH)[:, c, :, :])
            ins.then_inc(wT_ready, 1)

            def step(s, w, rnd):
                v = 1 - w
                if has(s, 0):
                    if not isinstance(s, int):
                        if w == 0:
                            for b in range(2, B):
                                dve.wait_ge(x_in[b], 16)
                    else:
                        dve.wait_ge(x_in[s // 2], 16)
                    for t in range(GT):
                        ins = dve.bn_stats(stats[:, w, t, :], x[:, bass.ds(s * GT + t, 1), :])
                    ins.then_inc(stats_done, 1)
                    wait_apart(dve, stats_done, s + 1, passed)
                    for t in range(GT):
                        ins = dve.bn_aggr(mv[:, w, t, :], stats[:, w, t, :])
                    ins.then_inc(mv_ready, 1)
                    dve.wait_ge(mv_ready, s + 1)
                    dve.tensor_scalar(veps[:, w, :], mv[:, w, :, 1], LN_EPS, None, ALU.add).then_inc(veps_ready, 1)
                if has(s, -1):
                    dve.wait_ge(rstd_ready, s)
                    if not isinstance(s, int) or s >= 3:
                        dve.wait_ge(zT_ps, s - 2)
                    for t in range(GT):
                        ins = dve.tensor_scalar(zn[:, v, t, :], x[:, bass.ds(s * GT + (t - GT), 1), :],
                                                mv[:, v, t, 0:1], rstd[:, v, t:t + 1], ALU.subtract, ALU.mult)
                    ins.then_inc(zn_ready, 1)
                if has(s, -2):
                    for qk in range(2):
                        dve.wait_ge(hi_ready, s * 2 + (qk - 3))
                        if not isinstance(s, int) or s >= 3:
                            dve.wait_ge(lo_ready, s * 2 + (qk - 5))
                        dve.tensor_tensor(rest[:, qk, :], ps_qk[:, w, qk, :], part[:, w, qk, 0, :],
                                          ALU.subtract).then_inc(rest_ready, 1)
                    for qk in range(2):
                        dve.wait_ge(mid_ready, s * 2 + (qk - 3))
                        dve.tensor_tensor(part[:, w, qk, 2, :], rest[:, qk, :], part[:, w, qk, 1, :],
                                          ALU.subtract).then_inc(lo_ready, 1)
            steps(dve, step)

        @block.tensor
        def _(pe):
            pe.wait_ge(w_in, 16)
            pe.wait_ge(masks, 4)
            for c in range(3):
                ins = pe.transpose(ps_qk[:, 0, 0, c * P:(c + 1) * P], w_rows[:, c, :], ident[:, :])
            ins.then_inc(wT_ps, 1)
            pe.wait_ge(wT_ready, 1)

            def step(s, w, rnd):
                v = 1 - w
                if has(s, -1):
                    if not isinstance(s, int) or s >= 3:
                        pe.wait_ge(zT_ready, s - 2)
                    pe.wait_ge(zn_ready, s)
                    for t in range(GT):
                        ins = pe.transpose(ps_T[:, v, t * P:(t + 1) * P], zn[:, v, t, :], ident[:, :])
                    ins.then_inc(zT_ps, 1)
                if has(s, -2):
                    pe.wait_ge(zT_ready, s - 1)
                    if not isinstance(s, int) or s >= 4:
                        pe.wait_ge(rest_ready, s * 2 - 6)
                        pe.wait_ge(v_ready, s - 3)
                    for qk in range(2):
                        pe.matmul(ps_qk[:, w, qk, :], wT[:, qk, :, :].rearrange("p h d -> p (h d)"),
                                  zT[:, w, :], start=True, stop=True).then_inc(qk_ps, 1)
                    for t in range(GT):
                        ins = pe.matmul(ps_v[:, w, t, :, :, :].rearrange("p m h d -> p (m h d)"), zT[:, w, t * P:(t + 1) * P],
                                        wT[:, 2, :, :].rearrange("p h d -> p (h d)"), start=True, stop=True)
                    ins.then_inc(v_ps, 1)
            steps(pe, step)


def phase_attention(nc, q_parts, k_parts, Wr, norm_w, f_norm, fWg, fWu, slots_in, tok_out, v_all, qo, ko,
                    x, gu_all, overflow, norms, ident, identb):
    with ExitStack() as ctx:
        def sb(name, shape, dt):
            return ctx.enter_context(nc.sbuf_tensor(name, shape, dt))

        def ps(name, shape, dt):
            return ctx.enter_context(nc.psum_tensor(name, shape, dt))

        def sem(name):
            return ctx.enter_context(nc.semaphore(name))

        EROWS = 4
        SFILLS = E * CAP // (P * EROWS)
        att = sb("att", [P, NPAIR, 2, TB, DH], F32)
        empty = sb("empty", [P, EROWS, ROW], F32)
        zeros = sb("zeros", [P, 2 * D], F32)
        vb = sb("vb", [P, 2, TB, 2, DH + 1], F32)
        prob = sb("prob", [P, PRING, 4, HALF], F32)
        avs = sb("avs", [P, HALF], F32)
        nmax = sb("nmax", [P, 2, 2 * TB], F32)
        nrest = sb("nrest", [P, 2, 2 * TB], F32)
        nparts = sb("nparts", [P, 2, NPART, TB], BF16)
        shift_rows = sb("shift_rows", [2 * NPART * TB, P], BF16)
        rden = sb("rden", [P, TB, 2], F32)
        pick = sb("pick", [P, 4, DH + 1], F32)

        norm_rows = sb("norm_rows", [E + 1, D], F32)
        fw_rows = sb("fw_rows", [P, 2 * F4], F32)
        rw = sb("rw", [P, RW], F32)
        before = sb("before", [P, P], BF16)
        ones = sb("ones", [P, P], BF16)
        iota_e = sb("iota_e", [P, E], F32)
        place = sb("place", [P, NT, 2], F32)
        carry = sb("carry", [P, E], F32)
        power = sb("power2", [P, TB], F32)
        send = sb("send", [P, TB, 2, ROW], F32)
        x2 = send[:, :, 0, 0:D]
        x2T = sb("x2T", [P, S], F32)
        junk = sb("junk", [P, TB, D], F32)
        stats = sb("stats2", [P, TB, 6], F32)
        mv = sb("mv2", [P, TB, 2], F32)
        veps = sb("veps2", [P, TB], F32)
        rstd = sb("rstd2", [P, TB], F32)
        ss = sb("ss", [P, TB], F32)
        meps = sb("meps", [P, TB], F32)
        rs = sb("rs", [P, TB], F32)
        logits = sb("logits", [P, TB, E], F32)
        ranked = sb("ranked", [P, TB, E], F32)
        index = sb("index", [P, TB, E], U32)
        chosen = sb("chosen", [P, TB, 2], F32)
        expo = sb("expo", [P, TB, E], F32)
        total = sb("total", [P, TB], F32)
        inv = sb("inv", [P, TB], F32)
        onehot = sb("onehot", [P, 2, TB, E], F32)
        given = sb("given", [P, TB, E], BF16)
        counts = sb("counts", [P, (TB + 1) * E], F32)
        gpos = sb("gpos", [P, TB, E], F32)
        mpos = sb("mpos", [P, 2, TB, E], F32)
        pos = sb("pos", [P, TB, 2], F32)
        keep = sb("keep", [P, TB, 2], F32)
        far = sb("far", [P, TB, 2], F32)
        both = sb("both", [P, TB], F32)
        slot = sb("slot", [P, TB, 2], F32)
        send_to = sb("send_to", [P, TB, 2], U32)

        ps_s = ps("ps_s", [P, 2, S], F32)
        ps_t = ps("ps_t", [P, 2, HALF], F32)
        ps_av = ps("ps_av", [P, HALF], F32)
        ps_m = ps("ps_m", [P, HALF], F32)
        M_NM = ps_m[0:2 * NPART * TB, 0:P // 2].bitcast(BF16)
        M_AV = ps_m[:, 128:128 + 4 * 4 * (DH + 1)].rearrange("p (c j i) -> p c j i", c=4, j=4)

        filled = sem("filled")
        fills_out = sem("fills_out")
        slots_filled = sem("slots_filled")
        loads = [sem(f"loads{u}") for u in range(QBUF)]
        shifts_in = [sem(f"shifts_in{u}") for u in range(QBUF)]
        pick_set = sem("pick_set")
        scores_ready = sem("scores_ready")
        scores_reduced = sem("scores_reduced")
        keyed_ready = sem("keyed_ready")
        prob_ready = sem("prob_ready")
        av_done = sem("av_done")
        av_copied = sem("av_copied")
        v_ready = sem("v_ready")
        nparts_ready = sem("nparts_ready")
        misc_ready = sem("misc_ready")
        result_taken = sem("result_taken")
        rows_copied = sem("rows_copied")
        pool_own = sem("pool_own")
        passed = sem("passed")
        rden_ready = sem("rden_ready")
        av_cleared = sem("av_cleared")

        w_in = sem("w_in2")
        pool_set = sem("pool_set")
        norms_ps = sem("norms_ps")
        norms_ready = sem("norms_ready")
        rw_ready = sem("rw_ready")
        result_added = sem("result_added")
        stats_done = sem("stats_done2")
        mv_ready = sem("mv_ready2")
        veps_ready = sem("veps_ready2")
        rstd_ready = sem("rstd_ready2")
        x2_ready = sem("x2_ready")
        x2_copied = sem("x2_copied")
        base_ready = sem("base_ready")
        ss_ready = sem("ss_ready")
        meps_ready = sem("meps_ready")
        rs_ready = sem("rs_ready")
        side_ready = sem("side_ready")
        side_taken = sem("side_taken")
        diff_ready = sem("diff_ready")
        expo_ready = sem("expo_ready")
        given_ready = sem("given_ready")
        send_ready = sem("send_ready")
        sent = sem("sent")
        dve_own = sem("dve_own2")
        carry_set = sem("carry_set")
        send_set = sem("send_set")
        passed2 = sem("passed2")

        block = ctx.enter_context(nc.Block())
        SIDE = 5
        SHARED_TILES = {4: (0, 1, 2), 5: (3, 4, 5), 6: (6, 7)}
        side_logits = ps_m[:, 0:TB * E].rearrange("p (t e) -> p t e", e=E)
        side_counts = ps_m[:, 0:(TB + 1) * E]

        def side_shared(r, t):
            c = P + (t - SHARED_TILES[r][0]) * 2 * F4
            return ps_m[:, c:c + 2 * F4]

        def steps(eng, step, route):
            for s in range(-2, 1):
                step(s, s % QBUF, s // QBUF, None)
            with eng.Fori(0, TB // QBUF) as i:
                for u in range(QBUF):
                    step(i * QBUF + (1 + u), (1 + u) % QBUF, i + (1 + u) // QBUF, None)
            with eng.Fori(1, B - 1) as b:
                for r in range(TB):
                    step(b * TB + (1 + r), (1 + r) % QBUF, b * (TB // QBUF) + (1 + r) // QBUF, (b - 1, r))
            for s in range(NPAIR - TB + 1, NPAIR + 1):
                step(s, s % QBUF, s // QBUF, (B - 2, s - (NPAIR - TB + 1)))
            for r in range(TB):
                route(B - 1, r)

        def has(s, offset):
            return has_item(s, offset, NPAIR)

        @block.sync
        def _(sp):
            def load(pair, u):
                for hd in range(2):
                    rows = bass.ds(pair * (2 * DH) + hd * DH, DH)
                    for i in range(NPART):
                        r = i * NPART * DH
                        sp.dma_start(qo[u][r:r + NPART * DH, hd, :],
                                     q_parts[i:i + 1, rows, :].broadcast_to((NPART, DH, S))).then_inc(loads[u], 16)
                        sp.dma_start(ko[u][r:r + NPART * DH, hd, :], k_parts[:, rows, :]).then_inc(loads[u], 16)

            def step(s, u, rnd, what):
                if isinstance(s, int) and s == -2:
                    for q in range(3):
                        load(q, q)
                    sp.dma_start(norm_rows[0:E, :], norm_w).then_inc(w_in, 16)
                    sp.dma_start(norm_rows[E:E + 1, :], f_norm.rearrange("(a d) -> a d", a=1)).then_inc(w_in, 16)
                    sp.dma_start(rw[:, 0:E], Wr).then_inc(w_in, 16)
                    sp.dma_start(fw_rows[:, 0:F4], fWg).then_inc(w_in, 16)
                    sp.dma_start(fw_rows[:, F4:2 * F4], fWu).then_inc(w_in, 16)
                if has(s, 3) and not (isinstance(s, int) and s + 3 < 3):
                    at_least(sp, keyed_ready, s * (4 * TB))
                    load(s + 3, (u + 3) % QBUF)
                if isinstance(s, int) and s in (-1, 0):
                    sp.wait_ge(filled, 2)
                    for c in range((s + 1) * SFILLS // 2, (s + 2) * SFILLS // 2):
                        r = c * P * EROWS
                        sp.dma_start(slots_in[r:r + P * EROWS, :].rearrange("(p r) d -> p r d", p=P),
                                     empty[:, :, :]).then_inc(slots_filled, 16)
                if has(s, 0):
                    sp.dma_start(tok_out[bass.ds(s * (2 * P), 2 * P), :].rearrange("(p r) d -> p (r d)", p=P),
                                 zeros[:, :]).then_inc(fills_out, 16)
                if has(s, 1):
                    sp.wait_ge(rows_copied, s + 2)
                    w = (u + 1) % QBUF
                    for hd in range(2):
                        sp.dma_start(qo[w][SHIFT:SHIFT + NPART, hd, :],
                                     shift_rows[hd * NPART * TB:(hd + 1) * NPART * TB, :]).then_inc(shifts_in[w], 16)
            steps(sp, step, lambda b, r: None)
            sp.wait_ge(fills_out, NPAIR * 16)

        @block.gpsimd
        def _(pool):
            pool.memset(zeros[:, :], 0.0).then_inc(filled, 1)
            pool.memset(empty[:, :, 0:D], 0.0)
            pool.memset(empty[:, :, D:ROW], float(FAR)).then_inc(filled, 1)
            pool.memset(pick[:, :, :], 0.0).then_inc(pick_set, 1)
            pool.wait_ge(pick_set, 1)
            pool.affine_select(out=pick[:, :, :], in_=pick[:, :, :], compare_op=ALU.not_equal, fill=1.0, base=0,
                               pattern=[[-32, 4], [-1, DH + 1]], channel_multiplier=1).then_inc(pick_set, 1)
            pool.memset(power[:, :], -0.5).then_inc(pool_set, 1)
            pool.memset(ones[:, :], 1.0).then_inc(pool_set, 1)
            pool.iota(iota_e[:, :], pattern=[[1, E]], base=0, channel_multiplier=0,
                      allow_small_or_imprecise_dtypes=True).then_inc(pool_set, 1)
            pool.iota(place[:, :, :], pattern=[[2 * P, NT], [1, 2]], base=0, channel_multiplier=2,
                      allow_small_or_imprecise_dtypes=True).then_inc(pool_set, 1)
            pool.wait_ge(pool_set, 4)
            pool.affine_select(out=before[:, :], in_=ones[:, :], compare_op=ALU.is_gt, fill=0.0, base=0,
                               pattern=[[1, P]], channel_multiplier=-1).then_inc(pool_set, 1)
            own = Chain(pool, pool_own)
            att_rows = att[:, :, :, :, :].rearrange("p m h t d -> p t (m h) d")
            x_rows = x[:, :, :].rearrange("p t (m d) -> p t m d", d=DH)

            def send_rows(times):
                pool.wait_ge(send_set, 1)
                pool.wait_ge(slots_filled, SFILLS * 16)
                wait_apart(pool, send_ready, times + 1, passed2)
                for t in range(TB):
                    for k in range(2):
                        pool.indirect_dma_start(
                            slots_in, bass.IndirectOffsetOnAxis(ap=send_to[:, t, k:k + 1], axis=0), send[:, t, k, :],
                            None, bounds_check=E * CAP - 1, oob_is_err=False).then_inc(sent, 16)

            def route(b, r):
                if r == 0:
                    wait_apart(pool, result_taken, b * TB + (TB + 1), passed2)
                    xb = x_rows[:, bass.ds(b * TB, TB), :, :]
                    pool.tensor_tensor(xb, xb, att_rows[:, :, bass.ds(b * H, H), :], ALU.add).then_inc(result_added, 1)
                    send_rows(b)
                if r == 1:
                    pool.wait_ge(veps_ready, b + 1)
                    pool.tensor_tensor(rstd[:, :], veps[:, :], power[:, :], ALU.pow).then_inc(rstd_ready, 1)
                if r == 3:
                    pool.wait_ge(meps_ready, b + 1)
                    pool.tensor_tensor(rs[:, :], meps[:, :], power[:, :], ALU.pow).then_inc(rs_ready, 1)
                    xf = x[:, bass.ds(b * TB, TB), :]
                    pool.tensor_tensor(xf, xf, x2, ALU.add).then_inc(base_ready, 1)

            def step(s, u, rnd, what):
                if what is not None:
                    route(*what)
                if has(s, 1):
                    if not isinstance(s, int) or s > 0:
                        wait_apart(pool, av_done, s * TB, passed)
                    pool.tensor_copy(vb[:, (u + 1) % 2, :, :, :], v_all[:, bass.ds(s + 1, 1), :, :, :]).then_inc(v_ready, 1)
                if has(s, 2):
                    pool.wait_ge(scores_reduced, s * (2 * TB) + 3 * 2 * TB)
                    if not isinstance(s, int) or s > -2:
                        wait_apart(pool, misc_ready, s + 2, passed)
                    m = nmax[:, u % 2, :].rearrange("p (h t) -> p h t", h=2)
                    r = nrest[:, :, :].rearrange("p a (h t) -> p a h t", h=2)
                    for ins in (lambda: pool.tensor_copy(nparts[:, :, 0, :], m),
                                lambda: pool.tensor_tensor(r[:, 0], m, nparts[:, :, 0, :], ALU.subtract),
                                lambda: pool.tensor_copy(nparts[:, :, 1, :], r[:, 0]),
                                lambda: pool.tensor_tensor(r[:, 1], r[:, 0], nparts[:, :, 1, :], ALU.subtract)):
                        ins().then_inc(pool_own, 1)
                        own.k += 1
                        wait_apart(pool, pool_own, s * 4 + (8 + (own.k - 1) % 4 + 1), passed)
                    pool.tensor_copy(nparts[:, :, 2, :], r[:, 1]).then_inc(nparts_ready, 1)
            steps(pool, step, route)
            send_rows(B)
            pool.wait_ge(sent, (B + 1) * TB * 2 * 16)

        @block.scalar
        def _(act):
            def route(b, r):
                if r == 1:
                    act.wait_ge(x2_ready, b + 1)
                    for t in range(TB):
                        ins = act.activation(junk[:, t, :], x2[:, t, :], ACT.Square, accum_out=ss[:, t:t + 1])
                    ins.then_inc(ss_ready, 1)
                    act.activation(send[:, :, 1, 0:D], x2, ACT.Copy).then_inc(x2_copied, 1)
                if r in (2, 3):
                    half = r - 2
                    act.wait_ge(side_ready, b * SIDE + (half + 1))
                    act.activation(x2T[:, half * HALF:(half + 1) * HALF], ps_m[:, :], ACT.Copy).then_inc(side_taken, 1)
                if r in (4, 5, 6):
                    act.wait_ge(side_ready, b * SIDE + (r - 1))
                    act.wait_ge(rs_ready, b + 1)
                    for t in SHARED_TILES[r]:
                        ins = act.activation(gu_all[:, bass.ds(b * TB + t, 1), :], side_shared(r, t), ACT.Copy,
                                             scale=rs[:, t:t + 1])
                    if r == 4:
                        ins = act.activation(logits[:, :, :], side_logits, ACT.Copy)
                    if r == 6:
                        ins = act.activation(counts[:, :], side_counts, ACT.Copy)
                    ins.then_inc(side_taken, 1)
                if r == 5:
                    act.wait_ge(diff_ready, b + 1)
                    act.activation(expo[:, :, :], expo[:, :, :], ACT.Exp).then_inc(expo_ready, 1)

            def step(s, u, rnd, what):
                def copy_av():
                    if has(s, -1):
                        act.wait_ge(av_done, s * TB)
                        at_least(act, misc_ready, s)
                        act.activation(avs[:, :], ps_av[:, :], ACT.Copy).then_inc(av_copied, 1)
                if has(s, 0):
                    for t in range(TB):
                        if not isinstance(s, int) or TB * s + t - PRING >= 0:
                            act.wait_ge(av_done, s * TB + (t - PRING + 1))
                        for j in range(4):
                            if t == 0 and j == 3:
                                copy_av()
                            if t == 6 and j == 2 and what is not None:
                                route(*what)
                            act.wait_ge(keyed_ready, s * (4 * TB) + (4 * t + j + 1))
                            act.activation(prob[:, t % PRING, j, :], ps_t[:, j % 2, :], ACT.Exp,
                                           scale=SOFTMAX_SCALE).then_inc(prob_ready, 1)
                else:
                    copy_av()
                    if what is not None:
                        route(*what)
            steps(act, step, route)

        @block.vector
        def _(dve):
            dve.memset(ps_av[:, :], 0.0).then_inc(av_cleared, 1)
            dve.memset(carry[:, :], 0.0).then_inc(carry_set, 1)
            dve.memset(send[:, :, :, :], 0.0).then_inc(send_set, 1)
            dve.memset(send_to[:, :, :], FAR).then_inc(send_ready, 1)
            dve.sem_inc(result_taken, 1)
            dve.sem_inc(side_taken, 1)
            own = Chain(dve, dve_own)
            CHAIN = 13

            def link(b, ins):
                own.k += 1
                ins.then_inc(dve_own, 1)
                dve.wait_ge(dve_own, b * CHAIN + ((own.k - 1) % CHAIN + 1))

            def route(b, r):
                at = bass.ds(b * TB, TB)
                if r == 0:
                    dve.wait_ge(result_added, b + 1)
                    for t in range(TB):
                        ins = dve.bn_stats(stats[:, t, :], x[:, bass.ds(b * TB + t, 1), :])
                    ins.then_inc(stats_done, 1)
                    wait_apart(dve, stats_done, b + 1, passed2)
                    for t in range(TB):
                        ins = dve.bn_aggr(mv[:, t, :], stats[:, t, :])
                    ins.then_inc(mv_ready, 1)
                    dve.wait_ge(mv_ready, b + 1)
                    dve.tensor_scalar(veps[:, :], mv[:, :, 1], LN_EPS, None, ALU.add).then_inc(veps_ready, 1)
                if r == 1:
                    dve.wait_ge(rstd_ready, b + 1)
                    dve.wait_ge(sent, b * (TB * 2 * 16) + TB * 2 * 16)
                    for t in range(TB):
                        ins = dve.tensor_scalar(x2[:, t, :], x[:, bass.ds(b * TB + t, 1), :], mv[:, t, 0:1],
                                                rstd[:, t:t + 1], ALU.subtract, ALU.mult)
                    ins.then_inc(x2_ready, 1)
                if r == 2:
                    dve.wait_ge(ss_ready, b + 1)
                    dve.tensor_scalar(meps[:, :], ss[:, :], 1.0 / D, RMS_EPS, ALU.mult, ALU.add).then_inc(meps_ready, 1)
                if r == 5:
                    dve.wait_ge(side_taken, b * SIDE + 4)
                    for t in range(TB):
                        if t == 0:
                            dve.sem_inc(passed2, 1)
                        ins = dve.max(ranked[:, t, :], logits[:, t, :])
                    link(b, ins)
                    dve.tensor_tensor(expo[:, :, :], ranked[:, :, :], ranked[:, :, 0:1].broadcast_to((P, TB, E)),
                                      ALU.subtract).then_inc(diff_ready, 1)
                    for t in range(TB):
                        ins = dve.max_index(index[:, t, :], ranked[:, t, :], logits[:, t, :])
                    link(b, ins)
                    link(b, dve.tensor_copy(chosen[:, :, :], index[:, :, 0:2]))
                    for k in range(2):
                        ins = dve.tensor_tensor(
                            onehot[:, k, :, :], iota_e[:, :].rearrange("p (a e) -> p a e", a=1).broadcast_to((P, TB, E)),
                            chosen[:, :, k:k + 1].broadcast_to((P, TB, E)), ALU.is_equal)
                    link(b, ins)
                    dve.tensor_tensor(given[:, :, :], onehot[:, 0, :, :], onehot[:, 1, :, :],
                                      ALU.add).then_inc(given_ready, 1)
                if r == 7:
                    dve.wait_ge(expo_ready, b + 1)
                    link(b, dve.tensor_reduce(total[:, :], expo[:, :, :], AX.X, ALU.add))
                    link(b, dve.reciprocal(inv[:, :], total[:, :]))
                    dve.wait_ge(x2_copied, b + 1)
                    dve.tensor_tensor(send[:, :, :, D + 1], expo[:, :, 0:2],
                                      inv[:, :].rearrange("p (t a) -> p t a", a=1).broadcast_to((P, TB, 2)), ALU.mult)
                    dve.wait_ge(side_taken, b * SIDE + 6)
                    link(b, dve.tensor_tensor(gpos[:, :, :], counts[:, 0:TB * E].rearrange("p (t e) -> p t e", e=E),
                                              carry[:, :].rearrange("p (a e) -> p a e", a=1).broadcast_to((P, TB, E)),
                                              ALU.add))
                    dve.tensor_tensor(carry[:, :], counts[:, TB * E:(TB + 1) * E], carry[:, :], ALU.add)
                    for k in range(2):
                        ins = dve.tensor_tensor(mpos[:, k, :, :], gpos[:, :, :], onehot[:, k, :, :], ALU.mult)
                    link(b, ins)
                    link(b, dve.tensor_reduce(pos[:, :, :].rearrange("p t k -> p k t"), mpos[:, :, :, :], AX.X, ALU.add))
                    link(b, dve.tensor_scalar(keep[:, :, :], pos[:, :, :], float(CAP), None, ALU.is_lt))
                    dve.tensor_tensor(both[:, :], keep[:, :, 0], keep[:, :, 1], ALU.mult)
                    dve.tensor_scalar(far[:, :, :], keep[:, :, :], -float(FAR), float(FAR), ALU.mult, ALU.add)
                    link(b, dve.scalar_tensor_tensor(out=slot[:, :, :], in0=chosen[:, :, :], scalar=float(CAP),
                                                     in1=pos[:, :, :], op0=ALU.mult, op1=ALU.add))
                    link(b, dve.tensor_scalar(overflow[:, at], both[:, :], -float(FAR), float(FAR), ALU.mult, ALU.add))
                    link(b, dve.tensor_tensor(send[:, :, :, D].bitcast(U32), place[:, at, :],
                                              overflow[:, at].rearrange("p (t a) -> p t a", a=1).broadcast_to((P, TB, 2)),
                                              ALU.add))
                    dve.tensor_tensor(send_to[:, :, :], slot[:, :, :], far[:, :, :], ALU.add).then_inc(send_ready, 1)

            def misc(s, u, rnd):
                dve.wait_ge(misc_ready, s + 2)
                if has(s, 1):
                    if not isinstance(s, int) or s >= 0:
                        dve.wait_ge(shifts_in[u], rnd * 32 + 32)
                    dve.tensor_copy(shift_rows[:, :], M_NM).then_inc(rows_copied, 1)
                if has(s, -1):
                    dve.reciprocal(rden4, M_AV[:, :, :, DH]).then_inc(rden_ready, 1)
                    dve.wait_ge(rden_ready, s)
                    for hd in range(2):
                        for half in range(2):
                            j = 2 * hd + half
                            ins = dve.tensor_tensor(
                                att[:, bass.ds(s - 1, 1), hd, 4 * half:4 * half + 4, :],
                                M_AV[:, :, j, 0:DH],
                                rden4[:, :, j:j + 1].broadcast_to((P, 4, DH)), ALU.mult)
                    ins.then_inc(result_taken, 1)

            rden4 = rden[:, :, :].rearrange("p t h -> p (t h)").rearrange("p (c j) -> p c j", j=4)

            def step(s, u, rnd, what):
                if has(s, 2):
                    at_least(dve, nparts_ready, s + 1 if not isinstance(s, int) or s > 0 else 0)
                    for k in range(2 * TB):
                        if k == 6 and not (isinstance(s, int) and s < -1):
                            misc(s, u, rnd)
                        if k == 9 and what is not None:
                            route(*what)
                        if k == 9 and isinstance(s, int) and s == 0:
                            dve.wait_ge(norms_ps, 1)
                            dve.tensor_copy(norms[:, :], ps_m[:, 0:E + 1]).then_inc(norms_ready, 1)
                            dve.wait_ge(w_in, 5 * 16)
                            dve.wait_ge(norms_ready, 1)
                            dve.tensor_scalar(rw[:, E:RW], fw_rows[:, :], norms[:, E:E + 1], None,
                                              ALU.mult).then_inc(rw_ready, 1)
                        dve.wait_ge(scores_ready, s * (2 * TB) + (4 * TB + k + 1))
                        dve.tensor_reduce(nmax[:, u % 2, k:k + 1], ps_s[:, k % 2, :], AX.X, ALU.max,
                                          negate=True).then_inc(scores_reduced, 1)
                else:
                    misc(s, u, rnd)
                    if what is not None:
                        route(*what)
            dve.wait_ge(pool_set, 4)
            dve.wait_ge(carry_set, 1)
            steps(dve, step, route)

        @block.tensor
        def _(pe):
            pe.wait_ge(pick_set, 2)
            pe.wait_ge(pool_set, 5)

            def scores_turn(s, u, k):
                w = (u + 2) % QBUF
                hd, t = k // TB, k % TB
                if not isinstance(s, int) or s > -2 or k >= 2:
                    pe.wait_ge(scores_reduced, s * (2 * TB) + (4 * TB + k - 1))
                for n in range(2):
                    ins = pe.matmul(ps_s[:, k % 2, n * HALF:(n + 1) * HALF], qo[w][0:SHIFT, hd, t * P:(t + 1) * P],
                                    ko[w][0:SHIFT, hd, n * HALF:(n + 1) * HALF], start=True, stop=True)
                ins.then_inc(scores_ready, 1)

            def keyed(s, u, t, j):
                hd, half = j // 2, j % 2
                if not isinstance(s, int) or s > 0 or 4 * t + j >= 2:
                    pe.wait_ge(prob_ready, s * (4 * TB) + (4 * t + j - 1))
                pe.matmul(ps_t[:, j % 2, :], ko[u][0:KROWS, hd, t * P:(t + 1) * P],
                          qo[u][0:KROWS, hd, half * HALF:(half + 1) * HALF], start=True, stop=True).then_inc(keyed_ready, 1)

            def values(s, u, t):
                pe.wait_ge(prob_ready, s * (4 * TB) + (4 * t + 4))
                if t == 0:
                    pe.wait_ge(v_ready, s + 1)
                    at_least(pe, av_copied, s)
                for j in range(4):
                    ins = pe.matmul(ps_av[32 * j:32 * j + DH + 1, :], vb[:, u % 2, t, j // 2, :],
                                    prob[:, t % PRING, j, :], start=(t == 0), stop=(t == TB - 1))
                ins.then_inc(av_done, 1)

            def side_turns(b, r):
                return b * SIDE + (min(max(r - 2, 0), SIDE) + 1)

            def route(b, r):
                if r not in (2, 3, 4, 5, 6):
                    return
                pe.wait_ge(side_taken, side_turns(b, r))
                if r in (2, 3):
                    wait_apart(pe, x2_ready, b + 1, passed2)
                    for t in range(4):
                        ins = pe.transpose(ps_m[:, t * P:(t + 1) * P], x2[:, 4 * (r - 2) + t, :], ident[:, :])
                    ins.then_inc(side_ready, 1)
                    return
                for t in SHARED_TILES[r]:
                    ins = pe.matmul(side_shared(r, t), x2T[:, t * P:(t + 1) * P], rw[:, E:RW], start=True, stop=True)
                if r == 4:
                    for t in range(TB):
                        ins = pe.matmul(side_logits[:, t, :], x2T[:, t * P:(t + 1) * P], rw[:, 0:E], start=True,
                                        stop=True)
                if r == 6:
                    pe.wait_ge(given_ready, b + 1)
                    pe.matmul(ps_m[:, 0:TB * E], before[:, :], given[:, :, :], start=True, stop=False,
                              skip_group_check=True)
                    for j in range(TB):
                        ins = pe.matmul(ps_m[:, (j + 1) * E:(TB + 1) * E].rearrange("p (t e) -> p t e", e=E), ones[:, :],
                                        given[:, j:j + 1, :].broadcast_to((P, TB - j, E)), start=False,
                                        stop=(j == TB - 1), skip_group_check=True)
                ins.then_inc(side_ready, 1)

            def misc(s, u, what):
                if has(s, 0):
                    at_least(pe, rows_copied, s + 1)
                if has(s, -2):
                    pe.wait_ge(result_taken, s)
                if not isinstance(s, int) or s > 0:
                    pe.wait_ge(rw_ready, 1)
                if what is not None:
                    pe.wait_ge(side_taken, side_turns(*what))
                if has(s, 1):
                    pe.wait_ge(nparts_ready, s + 2)
                if has(s, -1):
                    pe.wait_ge(av_copied, s)
                    for c in range(4):
                        ins = pe.matmul(M_AV[:, c, :, :].rearrange("p j i -> p (j i)"), avs[:, c * P:(c + 1) * P],
                                        pick[:, :, :].rearrange("p j i -> p (j i)"), start=True, stop=True)
                if has(s, 1):
                    ins = pe.transpose(M_NM, nparts[:, :, :, :].rearrange("p h a t -> p (h a t)"), identb[:, :])
                ins.then_inc(misc_ready, 1)

            def step(s, u, rnd, what):
                if has(s, 2):
                    w = (u + 2) % QBUF
                    pe.wait_ge(loads[w], (rnd + (u + 2) // QBUF) * 192 + 192)
                if has(s, 0):
                    pe.wait_ge(shifts_in[u], rnd * 32 + 32)
                for t in range(TB):
                    if has(s, 0):
                        keyed(s, u, t, 0)
                        keyed(s, u, t, 1)
                    if has(s, 2):
                        scores_turn(s, u, 2 * t)
                    if has(s, 0):
                        keyed(s, u, t, 2)
                    if t > 0 and has(s, 0):
                        values(s, u, t - 1)
                    elif t == 0 and has(s, -1):
                        values(s - 1, (u + 3) % QBUF, TB - 1)
                    if has(s, 0):
                        keyed(s, u, t, 3)
                    if has(s, 2):
                        scores_turn(s, u, 2 * t + 1)
                    if t == 2 and not (isinstance(s, int) and s < -1):
                        misc(s, u, what)
                    if t == 5 and what is not None and what[1] in (2, 3, 4, 5, 6):
                        if has(s, 1):
                            at_least(pe, rows_copied, s + 2)
                        pe.wait_ge(result_taken, s + 1)
                        route(*what)
                    if t == 3 and isinstance(s, int) and s == 0:
                        pe.wait_ge(w_in, 5 * 16)
                        pe.wait_ge(rows_copied, 2)
                        pe.transpose(ps_m[:, 0:E + 1], norm_rows[:, :], ident[0:E + 1, 0:E + 1]).then_inc(norms_ps, 1)
            pe.wait_ge(av_cleared, 1)
            steps(pe, step, route)


def phase_experts(nc, Wg, Wu, Wd, fWd, slots_in, tok_out, x, gu_all, overflow, norms, ident):
    with ExitStack() as ctx:
        def sb(name, shape, dt):
            return ctx.enter_context(nc.sbuf_tensor(name, shape, dt))

        def ps(name, shape, dt):
            return ctx.enter_context(nc.psum_tensor(name, shape, dt))

        def sem(name):
            return ctx.enter_context(nc.semaphore(name))

        NB = 2
        TE = NT // E
        wg = [sb(f"wg{w}", [P, F], F32) for w in range(NB)]
        wu = [sb(f"wu{w}", [P, F], F32) for w in range(NB)]
        wd = [sb(f"wd{w}", [P, FT, D], F32) for w in range(NB)]
        fwd = sb("fwd", [F4, D], F32)
        rows = sb("rows", [P, E, CT, ROW], F32)
        ysum = sb("ysum", [P, CT, D], F32)
        yrows = [sb(f"yrows{w}", [P, CT, D], F32) for w in range(NB)]
        yplace = [sb(f"yplace{w}", [P, CT], U32) for w in range(NB)]
        junk = sb("junk2", [P, CT, D], F32)
        ss = sb("ss2", [P, CT], F32)
        meps = sb("meps2", [P, CT], F32)
        rs = sb("rs2", [P, CT], F32)
        power = sb("power3", [P, CT], F32)
        h = sb("h", [P, CT, D], F32)
        hT = sb("hT", [P, CAP], F32)
        gelu = sb("gelu2", [P, FT, CAP], F32)
        gu = sb("gu2", [P, FT, CAP], F32)
        sh_gelu = sb("sh_gelu", [P, TE, F4], F32)
        sh_gu = sb("sh_gu", [P, TE, F4], F32)
        sh_guT = sb("sh_guT", [F4, TE * P], F32)
        sh_x = sb("sh_x", [P, TE, D], F32)
        zeros = sb("e_zeros", [P, TE, D], F32)
        room = sb("room", [P, TE], F32)
        ps_h = ps("ps_h", [P, CAP], F32)
        ps_g = ps("ps_g", [P, FT, CAP], F32)
        ps_u = ps("ps_u", [P, FT, CAP], F32)
        ps_y = ps("ps_y", [P, CT, D], F32)
        ps_shT = ps("ps_shT", [F4, TE * P], F32)
        ps_sh = ps("ps_sh", [P, TE, D], F32)

        fwd_in = sem("e_fwd_in")
        w_in = [sem(f"e_w_in{w}") for w in range(NB)]
        rows_in = [sem(f"e_rows_in{w}") for w in range(NB)]
        sent = [sem(f"e_sent{w}") for w in range(NB)]
        power_set = sem("e_power_set")
        ss_ready = sem("e_ss_ready")
        meps_ready = sem("e_meps_ready")
        rs_ready = sem("e_rs_ready")
        h_ready = sem("e_h_ready")
        turned = sem("e_turned")
        hT_ready = sem("e_hT_ready")
        gate_ps = sem("e_gate_ps")
        up_ps = sem("e_up_ps")
        gelu_ready = sem("e_gelu_ready")
        gu_ready = sem("e_gu_ready")
        down_ps = sem("e_down_ps")
        ysum_ready = sem("e_ysum_ready")
        y_ready = sem("e_y_ready")
        sh_gelu_ready = sem("sh_gelu_ready")
        sh_gu_ready = sem("sh_gu_ready")
        sh_turned = sem("sh_turned")
        sh_guT_ready = sem("sh_guT_ready")
        sh_down = sem("sh_down")
        sh_x_ready = sem("sh_x_ready")
        room_ready = sem("room_ready")
        sh_masked = sem("sh_masked")
        zeros_set = sem("e_zeros_set")
        passed2 = sem("e_passed2")
        sh_added = sem("sh_added")
        passed = sem("e_passed")

        block = ctx.enter_context(nc.Block())

        def steps(eng, step):
            run_steps(eng, step, -2, 1, 4, E + 1, NB)

        def has(s, offset):
            return has_item(s, offset, E)

        @block.sync
        def _(sp):
            def load_rows(e, w):
                sp.dma_start(rows[:, bass.ds(e, 1), :, :],
                             slots_in[bass.ds(e * CAP, CAP), :].rearrange("(t p) h -> p t h", p=P)).then_inc(rows_in[w], 16)

            def step(s, u, rnd):
                if isinstance(s, int) and s == -2:
                    load_rows(0, 0)
                    load_rows(1, 1)
                    sp.dma_start(fwd[:, :], fWd).then_inc(fwd_in, 16)
                if has(s, 3) and not (isinstance(s, int) and s < -1):
                    sp.wait_ge(ss_ready, s + 2)
                    load_rows(s + 3, (u + 1) % NB)
                if has(s, 1):
                    w = (u + 1) % NB
                    at_least(sp, down_ps, s)
                    e = bass.ds(s + 1, 1)
                    sp.dma_start(wg[w][:, :], Wg[e, :, :].rearrange("a h f -> h (a f)")).then_inc(w_in[w], 16)
                    sp.dma_start(wu[w][:, :], Wu[e, :, :].rearrange("a h f -> h (a f)")).then_inc(w_in[w], 16)
                    sp.dma_start(wd[w][:, :, :], Wd[e, :, :].rearrange("a (t p) h -> p (a t) h", p=P)).then_inc(w_in[w], 16)
            steps(sp, step)

        @block.gpsimd
        def _(pool):
            pool.memset(power[:, :], -0.5).then_inc(power_set, 1)
            pool.wait_ge(power_set, 1)

            def step(s, u, rnd):
                if has(s, 2):
                    pool.wait_ge(meps_ready, s + 3)
                    pool.tensor_tensor(rs[:, :], meps[:, :], power[:, :], ALU.pow).then_inc(rs_ready, 1)
                if has(s, -1):
                    w = (u + 1) % NB
                    wait_apart(pool, y_ready, s, passed)
                    for t in range(CT):
                        pool.indirect_dma_start(
                            tok_out, bass.IndirectOffsetOnAxis(ap=yplace[w][:, t:t + 1], axis=0), yrows[w][:, t, :],
                            None, bounds_check=2 * N - 1, oob_is_err=False).then_inc(sent[w], 16)
            steps(pool, step)
            for w in range(NB):
                pool.wait_ge(sent[w], E // NB * CT * 16)

        @block.scalar
        def _(act):
            def step(s, u, rnd):
                if has(s, -1):
                    act.wait_ge(sh_down, s)
                    at_least(act, sh_added, s - 1)
                    act.activation(sh_x[:, :, :], ps_sh[:, :, :], ACT.Copy).then_inc(sh_x_ready, 1)
                if has(s, 0):
                    act.wait_ge(gate_ps, s + 1)
                    at_least(act, gu_ready, s)
                    act.activation(gelu[:, :, :], ps_g[:, :, :], ACT.Gelu).then_inc(gelu_ready, 1)
                if has(s, 1):
                    at_least(act, sh_gu_ready, s + 1)
                    act.activation(sh_gelu[:, :, :], gu_all[:, bass.ds((s + 1) * TE, TE), 0:F4],
                                   ACT.Gelu).then_inc(sh_gelu_ready, 1)
                if has(s, 2):
                    act.wait_ge(rows_in[u], (rnd + 1) * 16 + 16)
                    at_least(act, meps_ready, s + 2)
                    for t in range(CT):
                        ins = act.activation(junk[:, t, :], rows[:, bass.ds(s + 2, 1), t, 0:D], ACT.Square,
                                             accum_out=ss[:, t:t + 1])
                    ins.then_inc(ss_ready, 1)
                if has(s, 0):
                    act.wait_ge(sh_turned, s + 1)
                    at_least(act, sh_down, s)
                    act.activation(sh_guT[:, :], ps_shT[:, :], ACT.Copy).then_inc(sh_guT_ready, 1)
                if has(s, 1):
                    act.wait_ge(turned, s + 2)
                    act.activation(hT[:, :], ps_h[:, :], ACT.Copy,
                                   scale=norms[:, bass.ds(s + 1, 1)]).then_inc(hT_ready, 1)
            steps(act, step)

        @block.vector
        def _(dve):
            dve.memset(zeros[:, :, :], 0.0).then_inc(zeros_set, 1)
            dve.wait_ge(zeros_set, 1)

            def per_slot(ap):
                return ap.broadcast_to((P, CT, D))

            def step(s, u, rnd):
                if has(s, -1):
                    at_least(dve, sh_added, s - 1)
                    dve.tensor_scalar(room[:, :], overflow[:, bass.ds((s - 1) * TE, TE)], 0.0, None,
                                      ALU.is_equal).then_inc(room_ready, 1)
                if has(s, 1):
                    dve.wait_ge(rs_ready, s + 2)
                    at_least(dve, turned, s + 1)
                    dve.tensor_tensor(h[:, :, :], rows[:, bass.ds(s + 1, 1), :, 0:D],
                                      per_slot(rs[:, :].rearrange("p (t a) -> p t a", a=1)), ALU.mult).then_inc(h_ready, 1)
                if has(s, 2):
                    dve.wait_ge(ss_ready, s + 3)
                    dve.tensor_scalar(meps[:, :], ss[:, :], 1.0 / D, RMS_EPS, ALU.mult, ALU.add).then_inc(meps_ready, 1)
                if has(s, 1):
                    dve.wait_ge(sh_gelu_ready, s + 2)
                    at_least(dve, sh_turned, s + 1)
                    dve.tensor_tensor(sh_gu[:, :, :], sh_gelu[:, :, :], gu_all[:, bass.ds((s + 1) * TE, TE), F4:2 * F4],
                                      ALU.mult).then_inc(sh_gu_ready, 1)
                if has(s, -1):
                    w = (u + 1) % NB
                    e = bass.ds(s - 1, 1)
                    dve.wait_ge(down_ps, s)
                    dve.tensor_tensor(ysum[:, :, :], ps_y[:, :, :], rows[:, e, :, 0:D], ALU.add).then_inc(ysum_ready, 1)
                    if has(s, -3) and not (isinstance(rnd, int) and s < 3):
                        at_least(dve, sent[w], (rnd + (u + 1) // NB - 1) * (CT * 16))
                    dve.tensor_copy(yplace[w][:, :], rows[:, e, :, D].bitcast(U32))
                    dve.wait_ge(ysum_ready, s)
                    dve.tensor_tensor(yrows[w][:, :, :], ysum[:, :, :], per_slot(rows[:, e, :, D + 1].rearrange("p a t -> p t a")),
                                      ALU.mult).then_inc(y_ready, 1)
                if has(s, 0):
                    dve.wait_ge(gelu_ready, s + 1)
                    dve.wait_ge(up_ps, s + 1)
                    dve.tensor_tensor(gu[:, :, :], gelu[:, :, :], ps_u[:, :, :], ALU.mult).then_inc(gu_ready, 1)
                if has(s, -1):
                    dve.wait_ge(sh_x_ready, s)
                    wait_apart(dve, room_ready, s, passed2)
                    dve.copy_predicated(sh_x[:, :, :], per_slot(room[:, :].bitcast(U32).rearrange("p (t a) -> p t a", a=1)),
                                        zeros[:, :, :]).then_inc(sh_masked, 1)
                    xt = x[:, bass.ds((s - 1) * TE, TE), :]
                    dve.wait_ge(sh_masked, s)
                    dve.tensor_tensor(xt, xt, sh_x[:, :, :], ALU.add).then_inc(sh_added, 1)
            steps(dve, step)

        @block.tensor
        def _(pe):
            def step(s, u, rnd):
                if has(s, 0):
                    pe.wait_ge(w_in[u], rnd * 48 + 48)
                    at_least(pe, gelu_ready, s)
                    pe.wait_ge(hT_ready, s + 1)
                    for f in range(FT):
                        ins = pe.matmul(ps_g[:, f, :], wg[u][:, f * P:(f + 1) * P], hT[:, :], start=True, stop=True)
                    ins.then_inc(gate_ps, 1)
                if has(s, -1):
                    w = (u + 1) % NB
                    at_least(pe, y_ready, s - 1) if not isinstance(s, int) or s > 1 else None
                    pe.wait_ge(gu_ready, s)
                    for t in range(CT):
                        for f in range(FT):
                            ins = pe.matmul(ps_y[:, t, :], gu[:, f, t * P:(t + 1) * P], wd[w][:, f, :],
                                            start=(f == 0), stop=(f == FT - 1))
                    ins.then_inc(down_ps, 1)
                if has(s, 0):
                    for f in range(FT):
                        ins = pe.matmul(ps_u[:, f, :], wu[u][:, f * P:(f + 1) * P], hT[:, :], start=True, stop=True)
                    ins.then_inc(up_ps, 1)
                    at_least(pe, sh_guT_ready, s)
                    wait_apart(pe, sh_gu_ready, s + 1, passed)
                    for t in range(TE):
                        ins = pe.transpose(ps_shT[:, t * P:(t + 1) * P], sh_gu[:, t, :], ident[:, :])
                    ins.then_inc(sh_turned, 1)
                if has(s, 1):
                    wait_apart(pe, h_ready, s + 2, passed)
                    for t in range(CT):
                        ins = pe.transpose(ps_h[:, t * P:(t + 1) * P], h[:, t, :], ident[:, :])
                    ins.then_inc(turned, 1)
                if has(s, 0):
                    at_least(pe, sh_x_ready, s)
                    pe.wait_ge(sh_guT_ready, s + 1)
                    for t in range(TE):
                        ins = pe.matmul(ps_sh[:, t, :], sh_guT[:, t * P:(t + 1) * P], fwd[:, :], start=True, stop=True)
                    ins.then_inc(sh_down, 1)
            pe.wait_ge(fwd_in, 16)
            steps(pe, step)


def phase_combine(nc, tok_out, x, out):
    with ExitStack() as ctx:
        def sb(name, shape, dt):
            return ctx.enter_context(nc.sbuf_tensor(name, shape, dt))

        def sem(name):
            return ctx.enter_context(nc.semaphore(name))

        TG = 4
        NG = NT // TG
        got = [sb(f"got{g}", [P, TG, 2, D], F32) for g in range(NG)]
        both_in = [sem(f"both_in{g}") for g in range(NG)]
        first_added = sem("first_added")
        rows_ready = sem("rows_ready")
        written = sem("written")

        block = ctx.enter_context(nc.Block())

        @block.sync
        def _(sp):
            for g in range(NG):
                first = g * TG * P * 2
                sp.dma_start(got[g][:, :, :, :].rearrange("p t k d -> p t (k d)"),
                             tok_out[first:first + TG * P * 2, :].rearrange("(t p k) d -> p t (k d)", p=P, k=2)
                             ).then_inc(both_in[g], 16)

        @block.vector
        def _(dve):
            for g in range(NG):
                xg = x[:, g * TG:(g + 1) * TG, :]
                dve.wait_ge(both_in[g], 16)
                dve.tensor_tensor(xg, xg, got[g][:, :, 0, :], ALU.add).then_inc(first_added, 1)
                dve.wait_ge(first_added, g + 1)
                dve.tensor_tensor(xg, xg, got[g][:, :, 1, :], ALU.add).then_inc(rows_ready, 1)

        @block.scalar
        def _(act):
            for g in range(NG):
                act.wait_ge(rows_ready, g + 1)
                b, t = g * TG // TB, g * TG % TB
                act.dma_start(out[b, t * P:(t + TG) * P, :].rearrange("(t p) d -> p t d", p=P),
                              x[:, g * TG:(g + 1) * TG, :]).then_inc(written, 16)
            act.wait_ge(written, NG * 16)


_INS = ['L0_attn_z', 'L0_attn_W_qkv', 'L0_ffn_Wr', 'L0_ffn_norm_w', 'L0_ffn_Wg', 'L0_ffn_Wu', 'L0_ffn_Wd',
        'L0_ffn_f_norm', 'L0_ffn_fWg', 'L0_ffn_fWu', 'L0_ffn_fWd']
_OUTS = [((B, S, D), 'float32')]


def kernel(**inputs):
    import numpy as _np
    import concourse.bacc as _bacc
    from concourse import mybir as _mybir
    from concourse.bass_utils import run_bass_kernel_spmd as _run

    nc = _bacc.Bacc("TRN2", target_bir_lowering=False, num_devices=1)
    arrays, args = {}, []
    for name in _INS:
        a = _np.ascontiguousarray(inputs[name])
        arrays[f"in_{name}_dram"] = a
        args.append(nc.dram_tensor(f"in_{name}_dram", a.shape, _mybir.dt.from_np(a.dtype), kind="ExternalInput").ap())
    for i, (shape, dtype) in enumerate(_OUTS):
        dt = _mybir.dt.from_np(_np.dtype(dtype))
        args.append(nc.dram_tensor(f"out_{i}_dram", shape, dt, kind="ExternalOutput").ap())
    attention_moe(nc, *args)
    r = _run(nc, [arrays], core_ids=[0])
    return r.results[0]["out_0_dram"]
```

```python
from contextlib import ExitStack

import concourse.bass as bass
from concourse import mybir

F32 = mybir.dt.float32
BF16 = mybir.dt.bfloat16
U32 = mybir.dt.uint32
ALU = mybir.AluOpType
ACT = mybir.ActivationFunctionType
AX = mybir.AxisListType

P = 128
B, S, D = 4, 1024, 128
N = B * S
H, DH = 16, 8
NPAIR = B * H // 2
TB = S // P
NT = N // P
HALF = 512
NPART = 3
PROD = NPART * NPART * DH
SHIFT = 96
KROWS = SHIFT + NPART
QBUF = 4
PRING = 4
E = 8
CAP = 512
assert E * CAP == NPAIR * P and N == NPAIR * P
CT = CAP // P
F = 256
FT = F // P
F4 = 64
ROW = D + 2
RW = E + 2 * F4
LN_EPS = 1e-5
RMS_EPS = 1e-6
SOFTMAX_SCALE = float(DH) ** -0.5
FAR = 1 << 16


def wait_apart(eng, semaphore, value, passed):
    eng.wait_ge(semaphore, value)
    eng.sem_inc(passed, 1)


def run_steps(eng, step, start, first, last, stop, unroll):
    for s in range(start, first):
        step(s, s % unroll, s // unroll)
    assert (last - first + 1) % unroll == 0
    with eng.Fori(0, (last - first + 1) // unroll) as i:
        for u in range(unroll):
            step(i * unroll + (first + u), (first + u) % unroll, i + (first + u) // unroll)
    for s in range(last + 1, stop):
        step(s, s % unroll, s // unroll)


def has_item(s, offset, n):
    return not isinstance(s, int) or 0 <= s + offset < n


def at_least(eng, semaphore, value):
    if not isinstance(value, int) or value > 0:
        eng.wait_ge(semaphore, value)


def attention_moe(nc, z, W_qkv, Wr, norm_w, Wg, Wu, Wd, f_norm, fWg, fWu, fWd, out, debug=None):
    with ExitStack() as ctx:
        def sb(name, shape, dt):
            return ctx.enter_context(nc.sbuf_tensor(name, shape, dt))

        q_parts = nc.dram_tensor("q_parts", (NPART, NPAIR * 2 * DH, S), BF16, kind="Internal").ap()
        k_parts = nc.dram_tensor("k_parts", (NPART, NPAIR * 2 * DH, S), BF16, kind="Internal").ap()
        slots_in = nc.dram_tensor("slots_in", (E * CAP, ROW), F32, kind="Internal").ap()
        tok_out = nc.dram_tensor("tok_out", (N * 2, D), F32, kind="Internal").ap()

        x = sb("x", [P, NT, D], F32)
        ident = sb("ident", [P, P], F32)
        identb = sb("identb", [P, P], BF16)
        qo = [sb(f"qo{u}", [P, 2, S], BF16) for u in range(QBUF)]
        ko = [sb(f"ko{u}", [P, 2, S], BF16) for u in range(QBUF)]
        v_all = sb("v_all", [P, NPAIR, TB, 2, DH + 1], F32)
        gu_all = sb("gu_all", [P, NT, 2 * F4], F32)
        overflow = sb("overflow", [P, NT], F32)
        norms = sb("norms", [P, E + 1], F32)
        loads = [ctx.enter_context(nc.semaphore(f"loads{u}")) for u in range(QBUF)]

        phase_qkv(nc, z, W_qkv, q_parts, k_parts, x, v_all, qo, ko, loads, ident, identb)
        phase_attention(nc, q_parts, k_parts, Wr, norm_w, f_norm, fWg, fWu, fWd, slots_in, tok_out, v_all, qo, ko, loads,
                        x, gu_all, overflow, norms, ident, identb)
        phase_experts(nc, Wg, Wu, Wd, slots_in, tok_out, norms, ident)
        phase_combine(nc, tok_out, x, out)


def load_pair(eng, pair, u, qo, ko, q_parts, k_parts, loads, heads=(0, 1)):
    for hd in heads:
        rows = bass.ds(pair * (2 * DH) + hd * DH, DH)
        for i in range(NPART):
            r = i * NPART * DH
            eng.dma_start(qo[u][r:r + NPART * DH, hd, :],
                          q_parts[i:i + 1, rows, :].broadcast_to((NPART, DH, S))).then_inc(loads[u], 16)
            eng.dma_start(ko[u][r:r + NPART * DH, hd, :], k_parts[:, rows, :]).then_inc(loads[u], 16)


def phase_qkv(nc, z, W_qkv, q_parts, k_parts, x, v_all, qo, ko, loads, ident, identb):
    GT = 4
    G = NT // GT
    GC = GT * P
    assert GC == HALF
    with ExitStack() as ctx:
        def sb(name, shape, dt):
            return ctx.enter_context(nc.sbuf_tensor(name, shape, dt))

        def ps(name, shape, dt):
            return ctx.enter_context(nc.psum_tensor(name, shape, dt))

        def sem(name):
            return ctx.enter_context(nc.semaphore(name))

        w_rows = sb("w_rows", [P, 3, D], F32)
        wT = sb("wT", [P, 3, H, DH], F32)
        zn = sb("zn", [P, 2, GT, D], F32)
        zT = sb("zT", [P, 2, GC], F32)
        stats = sb("stats", [P, 2, GT, 6], F32)
        mv = sb("mv", [P, 2, GT, 2], F32)
        veps = sb("veps", [P, 2, GT], F32)
        power = sb("power", [P, GT], F32)
        rstd = sb("rstd", [P, 2, GT], F32)
        part = sb("part", [P, 2, 2, NPART, GC], BF16)
        rest = sb("rest", [P, 2, GC], F32)

        ps_T = ps("ps_T", [P, 2, GC], F32)
        ps_qk = ps("ps_qk", [P, 2, 2, GC], F32)
        ps_v = ps("ps_v", [P, 2, GT, H // 2, 2, DH], F32)

        x_in = [sem(f"x_in{b}") for b in range(B)]
        w_in = sem("w_in")
        masks = sem("masks")
        passed2 = sem("passed_pool")
        zeros_set = sem("zeros_set")
        ones_set = sem("ones_set")
        wT_ps = sem("wT_ps")
        wT_ready = sem("wT_ready")
        stats_done = sem("stats_done")
        mv_ready = sem("mv_ready")
        veps_ready = sem("veps_ready")
        rstd_ready = sem("rstd_ready")
        zn_ready = sem("zn_ready")
        zT_ps = sem("zT_ps")
        zT_ready = sem("zT_ready")
        qk_ps = sem("qk_ps")
        v_ps = sem("v_ps")
        hi_ready = sem("hi_ready")
        rest_ready = sem("rest_ready")
        mid_ready = sem("mid_ready")
        lo_ready = sem("lo_ready")
        v_ready = sem("v_ready")
        parts_out = [sem(f"parts_out{w}") for w in range(2)]
        passed = sem("passed0")

        block = ctx.enter_context(nc.Block())

        def steps(eng, step):
            run_steps(eng, step, 0, 4, G - 1, G + 2, 2)

        def has(s, offset):
            return has_item(s, offset, G)

        @block.sync
        def _(sp):
            for b in range(B):
                if b == 1:
                    sp.dma_start(w_rows[:, :, :], W_qkv.rearrange("(c p) d -> p c d", p=P)).then_inc(w_in, 16)
                sp.dma_start(x[:, b * TB:(b + 1) * TB, :], z[b].rearrange("(t p) d -> p t d", p=P)).then_inc(x_in[b], 16)

            def step(s, w, rnd):
                if isinstance(s, int) and s >= G:
                    for v in range(2):
                        sp.wait_ge(parts_out[v], 2 * 16)
                    sp.wait_ge(ones_set, QBUF)
                    sp.wait_ge(zeros_set, 2)
                    load_pair(sp, 0, 0, qo, ko, q_parts, k_parts, loads, heads=(s - G,))
                if has(s, -2):
                    for qk, store in enumerate((q_parts, k_parts)):
                        sp.wait_ge(lo_ready, s * 2 + (qk - 3))
                        sp.dma_start(store[:, bass.ds((rnd - 1) * P, P), w * GC:(w + 1) * GC].rearrange("i p s -> p i s"),
                                     part[:, w, qk, :, :]).then_inc(parts_out[w], 16)
            steps(sp, step)
            for w in range(2):
                sp.wait_ge(parts_out[w], (G // 2) * 2 * 16)

        @block.gpsimd
        def _(pool):
            pool.memset(ident[:, :], 0.0).then_inc(masks, 1)
            pool.memset(identb[:, :], 0.0).then_inc(masks, 1)
            pool.wait_ge(masks, 2)
            for m in (ident, identb):
                pool.affine_select(out=m[:, :], in_=m[:, :], compare_op=ALU.not_equal, fill=1.0, base=0,
                                   pattern=[[-1, P]], channel_multiplier=1).then_inc(masks, 1)
            pool.memset(power[:, :], -0.5).then_inc(masks, 1)
            pool.wait_ge(masks, 5)
            for u in range(QBUF):
                pool.memset(ko[u][SHIFT:P, :, :], 1.0).then_inc(ones_set, 1)
            pool.wait_ge(ones_set, QBUF)

            def step(s, w, rnd):
                if has(s, 0):
                    pool.wait_ge(veps_ready, s + 1)
                    pool.tensor_tensor(rstd[:, w, :], veps[:, w, :], power[:, :], ALU.pow).then_inc(rstd_ready, 1)
                if has(s, -2):
                    for qk in range(2):
                        wait_apart(pool, mid_ready, s * 2 + (qk - 3), passed2)
                        pool.tensor_tensor(part[:, w, qk, 2, :], rest[:, qk, :], part[:, w, qk, 1, :],
                                           ALU.subtract).then_inc(lo_ready, 1)
                if isinstance(s, int) and s == QBUF - 1:
                    pool.wait_ge(lo_ready, 2 * (s - 1))
                    pool.memset(v_all[:, :, :, :, DH:DH + 1], 1.0).then_inc(ones_set, 1)
                    pool.wait_ge(ones_set, QBUF + 1)
            steps(pool, step)

        @block.scalar
        def _(act):
            def step(s, w, rnd):
                v = 1 - w
                if has(s, -2):
                    for qk in range(2):
                        act.wait_ge(qk_ps, s * 2 + (qk - 3))
                        if not isinstance(s, int) or s >= 4:
                            act.wait_ge(parts_out[w], rnd * (2 * 16) - (2 * 16))
                        act.activation(part[:, w, qk, 0, :], ps_qk[:, w, qk, :], ACT.Copy).then_inc(hi_ready, 1)
                    act.wait_ge(v_ps, s - 1)
                    for t in range(GT):
                        ins = act.activation(v_all[:, bass.ds((rnd - 1) * (H // 2), H // 2), w * GT + t, :, 0:DH],
                                             ps_v[:, w, t, :, :, :], ACT.Copy)
                    ins.then_inc(v_ready, 1)
                if has(s, -1):
                    act.wait_ge(zT_ps, s)
                    act.activation(zT[:, v, :], ps_T[:, v, :], ACT.Copy).then_inc(zT_ready, 1)
                if has(s, -2):
                    for qk in range(2):
                        act.wait_ge(rest_ready, s * 2 + (qk - 3))
                        act.activation(part[:, w, qk, 1, :], rest[:, qk, :], ACT.Copy).then_inc(mid_ready, 1)
            steps(act, step)

        @block.vector
        def _(dve):
            def clear(u):
                dve.memset(qo[u][64:P, :, :], 0.0).then_inc(zeros_set, 1)
                dve.memset(ko[u][64:SHIFT, :, :], 0.0).then_inc(zeros_set, 1)

            clear(0)
            dve.wait_ge(wT_ps, 1)
            for c in range(3):
                ins = dve.tensor_copy(wT[:, c, :, :], ps_qk[:, 0, 0, 0:3 * P].rearrange(
                    "p (h c d) -> p c h d", c=3, d=DH)[:, c, :, :])
            ins.then_inc(wT_ready, 1)

            def step(s, w, rnd):
                v = 1 - w
                if has(s, 0):
                    if not isinstance(s, int):
                        if w == 0:
                            for b in range(2, B):
                                dve.wait_ge(x_in[b], 16)
                    else:
                        dve.wait_ge(x_in[s // 2], 16)
                    for t in range(GT):
                        ins = dve.bn_stats(stats[:, w, t, :], x[:, bass.ds(s * GT + t, 1), :])
                    ins.then_inc(stats_done, 1)
                    wait_apart(dve, stats_done, s + 1, passed)
                    for t in range(GT):
                        ins = dve.bn_aggr(mv[:, w, t, :], stats[:, w, t, :])
                    ins.then_inc(mv_ready, 1)
                    dve.wait_ge(mv_ready, s + 1)
                    dve.tensor_scalar(veps[:, w, :], mv[:, w, :, 1], LN_EPS, None, ALU.add).then_inc(veps_ready, 1)
                if has(s, -1):
                    dve.wait_ge(rstd_ready, s)
                    if not isinstance(s, int) or s >= 3:
                        dve.wait_ge(zT_ps, s - 2)
                    for t in range(GT):
                        ins = dve.tensor_scalar(zn[:, v, t, :], x[:, bass.ds(s * GT + (t - GT), 1), :],
                                                mv[:, v, t, 0:1], rstd[:, v, t:t + 1], ALU.subtract, ALU.mult)
                    ins.then_inc(zn_ready, 1)
                if has(s, -2):
                    for qk in range(2):
                        dve.wait_ge(hi_ready, s * 2 + (qk - 3))
                        if not isinstance(s, int) or s >= 3:
                            dve.wait_ge(lo_ready, s * 2 + (qk - 5))
                        dve.tensor_tensor(rest[:, qk, :], ps_qk[:, w, qk, :], part[:, w, qk, 0, :],
                                          ALU.subtract).then_inc(rest_ready, 1)
                if isinstance(s, int) and s >= G:
                    for u in ((1, 2) if s == G else (3,)):
                        clear(u)
            steps(dve, step)

        @block.tensor
        def _(pe):
            pe.wait_ge(w_in, 16)
            pe.wait_ge(masks, 4)
            for c in range(3):
                ins = pe.transpose(ps_qk[:, 0, 0, c * P:(c + 1) * P], w_rows[:, c, :], ident[:, :])
            ins.then_inc(wT_ps, 1)
            pe.wait_ge(wT_ready, 1)

            def step(s, w, rnd):
                v = 1 - w
                if has(s, -2):
                    pe.wait_ge(zT_ready, s - 1)
                    if not isinstance(s, int) or s >= 4:
                        pe.wait_ge(rest_ready, s * 2 - 6)
                        pe.wait_ge(v_ready, s - 3)
                    for qk in range(2):
                        pe.matmul(ps_qk[:, w, qk, :], wT[:, qk, :, :].rearrange("p h d -> p (h d)"),
                                  zT[:, w, :], start=True, stop=True).then_inc(qk_ps, 1)
                    for t in range(GT):
                        ins = pe.matmul(ps_v[:, w, t, :, :, :].rearrange("p m h d -> p (m h d)"), zT[:, w, t * P:(t + 1) * P],
                                        wT[:, 2, :, :].rearrange("p h d -> p (h d)"), start=True, stop=True)
                    ins.then_inc(v_ps, 1)
                if has(s, -1):
                    if not isinstance(s, int) or s >= 3:
                        pe.wait_ge(zT_ready, s - 2)
                    pe.wait_ge(zn_ready, s)
                    for t in range(GT):
                        ins = pe.transpose(ps_T[:, v, t * P:(t + 1) * P], zn[:, v, t, :], ident[:, :])
                    ins.then_inc(zT_ps, 1)
            steps(pe, step)


def phase_attention(nc, q_parts, k_parts, Wr, norm_w, f_norm, fWg, fWu, fWd, slots_in, tok_out, v_all, qo, ko, loads,
                    x, gu_all, overflow, norms, ident, identb):
    with ExitStack() as ctx:
        def sb(name, shape, dt):
            return ctx.enter_context(nc.sbuf_tensor(name, shape, dt))

        def ps(name, shape, dt):
            return ctx.enter_context(nc.psum_tensor(name, shape, dt))

        def sem(name):
            return ctx.enter_context(nc.semaphore(name))

        EROWS = 4
        SFILLS = E * CAP // (P * EROWS)
        att = sb("att", [P, NPAIR, 2, TB, DH], F32)
        empty = sb("empty", [P, EROWS, ROW], F32)
        zeros = sb("zeros", [P, 2 * D], F32)
        vb = sb("vb", [P, 2, TB, 2, DH + 1], F32)
        prob = sb("prob", [P, PRING, 4, HALF], F32)
        avs = sb("avs", [3 * 32 + DH + 1, HALF], F32)
        nmax = sb("nmax", [P, 2, 2 * TB], F32)
        nrest = sb("nrest", [P, 2, 2 * TB], F32)
        nparts = sb("nparts", [P, 2, NPART, TB], BF16)
        shift_rows = sb("shift_rows", [2 * NPART * TB, P], BF16)
        rden = sb("rden", [P, TB, 2], F32)

        norm_rows = sb("norm_rows", [E + 1, D], F32)
        fw_rows = sb("fw_rows", [P, 2 * F4], F32)
        rw = sb("rw", [P, RW], F32)
        before = sb("before", [P, P], BF16)
        ones = sb("ones", [P, P], BF16)
        iota_e = sb("iota_e", [P, E], F32)
        place = sb("place", [P, NT, 2], F32)
        carry = sb("carry", [P, E], F32)
        power = sb("power2", [P, TB], F32)
        sends = [sb(f"send{w}", [P, TB, 2, ROW], F32) for w in range(2)]
        x2T = sb("x2T", [P, S], F32)
        junk = sb("junk", [P, TB, D], F32)
        stats = sb("stats2", [P, TB, 6], F32)
        mv = sb("mv2", [P, TB, 2], F32)
        veps = sb("veps2", [P, TB], F32)
        rstd = sb("rstd2", [P, TB], F32)
        ss = sb("ss", [P, TB], F32)
        meps = sb("meps", [P, TB], F32)
        rs = sb("rs", [P, TB], F32)
        logits = sb("logits", [P, TB, E], F32)
        ranked = sb("ranked", [P, TB, E], F32)
        index = sb("index", [P, TB, E], U32)
        chosen = sb("chosen", [P, TB, 2], F32)
        expo = sb("expo", [P, TB, E], F32)
        total = sb("total", [P, TB], F32)
        inv = sb("inv", [P, TB], F32)
        onehot = sb("onehot", [P, 2, TB, E], F32)
        given = sb("given", [P, TB, E], BF16)
        counts = sb("counts", [P, (TB + 1) * E], F32)
        gpos = sb("gpos", [P, TB, E], F32)
        mpos = sb("mpos", [P, 2, TB, E], F32)
        pos = sb("pos", [P, TB, 2], F32)
        keep = sb("keep", [P, TB, 2], F32)
        far = sb("far", [P, TB, 2], F32)
        both = sb("both", [P, TB], F32)
        slot = sb("slot", [P, TB, 2], F32)
        send_to = [sb(f"send_to{w}", [P, TB, 2], U32) for w in range(2)]

        TG = 4
        NG = NT // TG
        fwd = sb("fwd", [F4, D], F32)
        sh_gelu = sb("sh_gelu", [P, TG, F4], F32)
        sh_gu = sb("sh_gu", [P, TG, F4], F32)
        sh_guT = sb("sh_guT", [F4, 2, TG * P], F32)
        sh_x = sb("sh_x", [P, TG, D], F32)
        room = sb("room", [P, TG], F32)

        ps_s = ps("ps_s", [P, 2, S], F32)
        ps_t = ps("ps_t", [P, 2, HALF], F32)
        ps_av = ps("ps_av", [P, HALF], F32)
        ps_m = ps("ps_m", [P, HALF], F32)
        M_NM = ps_m[0:2 * NPART * TB, 0:P // 2].bitcast(BF16)
        AVR = 3 * 32 + DH + 1
        M_AV = ps_m[:, P // 2:P // 2 + 4 * AVR].rearrange("p (c r) -> p c r", c=4)

        filled = sem("filled")
        fills_out = sem("fills_out")
        slots_filled = sem("slots_filled")
        shifts_in = [sem(f"shifts_in{u}") for u in range(QBUF)]
        scores_ready = sem("scores_ready")
        scores_reduced = sem("scores_reduced")
        keyed_ready = sem("keyed_ready")
        prob_ready = sem("prob_ready")
        av_done = sem("av_done")
        av_copied = sem("av_copied")
        v_ready = sem("v_ready")
        nparts_ready = sem("nparts_ready")
        misc_ready = sem("misc_ready")
        result_taken = sem("result_taken")
        rows_copied = sem("rows_copied")
        pool_own = sem("pool_own")
        passed = sem("passed")
        rden_ready = sem("rden_ready")
        av_cleared = sem("av_cleared")

        w_in = sem("w_in2")
        pool_set = sem("pool_set")
        norms_ps = sem("norms_ps")
        norms_ready = sem("norms_ready")
        rw_ready = sem("rw_ready")
        result_added = sem("result_added")
        stats_done = sem("stats_done2")
        mv_ready = sem("mv_ready2")
        veps_ready = sem("veps_ready2")
        rstd_ready = sem("rstd_ready2")
        x2_ready = sem("x2_ready")
        x2_copied = sem("x2_copied")
        base_ready = sem("base_ready")
        ss_ready = sem("ss_ready")
        meps_ready = sem("meps_ready")
        rs_ready = sem("rs_ready")
        side_ready = sem("side_ready")
        side_taken = sem("side_taken")
        diff_ready = sem("diff_ready")
        expo_ready = sem("expo_ready")
        given_ready = sem("given_ready")
        send_ready = sem("send_ready")
        sent = sem("sent")
        dve_own = sem("dve_own2")
        carry_set = sem("carry_set")
        send_set = sem("send_set")
        passed2 = sem("passed2")

        sh_gelu_ready = sem("sh_gelu_ready")
        sh_gu_ready = sem("sh_gu_ready")
        sh_turned = sem("sh_turned")
        sh_guT_ready = sem("sh_guT_ready")
        sh_down = sem("sh_down")
        sh_x_ready = sem("sh_x_ready")
        room_ready = sem("room_ready")
        sh_masked = sem("sh_masked")
        sh_added = sem("sh_added")

        block = ctx.enter_context(nc.Block())

        def shared_steps(eng, step):
            run_steps(eng, step, -1, 1, NG - 2, NG + 1, 2)

        def has_group(g, offset):
            return has_item(g, offset, NG)

        def which(b):
            w = int(isinstance(b, int) and b == B - 1)
            return w, sends[w], sends[w][:, :, 0, 0:D]

        SIDE = 6
        ROUTED = {3: (0, 3), 4: (3, 6), 5: (6, TB)}

        def steps(eng, step, route, PARTS=TB):
            for s in range(-2, 1):
                step(s, s % QBUF, s // QBUF, None)
            with eng.Fori(0, TB // QBUF) as i:
                for u in range(QBUF):
                    step(i * QBUF + (1 + u), (1 + u) % QBUF, i + (1 + u) // QBUF, None)
            with eng.Fori(1, B - 1) as b:
                for r in range(TB):
                    step(b * TB + (1 + r), (1 + r) % QBUF, b * (TB // QBUF) + (1 + r) // QBUF, (b - 1, r))
            for s in range(NPAIR - TB + 1, NPAIR + 1):
                step(s, s % QBUF, s // QBUF, (B - 2, s - (NPAIR - TB + 1)))
            for r in range(TB):
                for part in range(PARTS):
                    route(B - 1, r, part)

        def has(s, offset):
            return has_item(s, offset, NPAIR)

        @block.sync
        def _(sp):
            def load(pair, u):
                load_pair(sp, pair, u, qo, ko, q_parts, k_parts, loads)

            def step(s, u, rnd, what):
                if isinstance(s, int) and s == -2:
                    load(1, 1)
                    load(2, 2)
                    sp.dma_start(norm_rows[0:E, :], norm_w).then_inc(w_in, 16)
                    sp.dma_start(norm_rows[E:E + 1, :], f_norm.rearrange("(a d) -> a d", a=1)).then_inc(w_in, 16)
                    sp.dma_start(rw[:, 0:E], Wr).then_inc(w_in, 16)
                    sp.dma_start(fw_rows[:, 0:F4], fWg).then_inc(w_in, 16)
                    sp.dma_start(fw_rows[:, F4:2 * F4], fWu).then_inc(w_in, 16)
                    sp.dma_start(fwd[:, :], fWd).then_inc(w_in, 16)
                if has(s, 3) and not (isinstance(s, int) and s + 3 < 3):
                    at_least(sp, keyed_ready, s * (4 * TB))
                    load(s + 3, (u + 3) % QBUF)
                if isinstance(s, int) and s in (-1, 0):
                    sp.wait_ge(filled, 2)
                    for c in range((s + 1) * SFILLS // 2, (s + 2) * SFILLS // 2):
                        r = c * P * EROWS
                        sp.dma_start(slots_in[r:r + P * EROWS, :].rearrange("(p r) d -> p r d", p=P),
                                     empty[:, :, :]).then_inc(slots_filled, 16)
                if has(s, 0):
                    sp.dma_start(tok_out[bass.ds(s * (2 * P), 2 * P), :].rearrange("(p r) d -> p (r d)", p=P),
                                 zeros[:, :]).then_inc(fills_out, 16)
                if has(s, 1):
                    sp.wait_ge(rows_copied, s + 2)
                    w = (u + 1) % QBUF
                    for hd in range(2):
                        sp.dma_start(qo[w][SHIFT:SHIFT + NPART, hd, :],
                                     shift_rows[hd * NPART * TB:(hd + 1) * NPART * TB, :]).then_inc(shifts_in[w], 16)
            steps(sp, step, lambda b, r, part: None)
            sp.wait_ge(fills_out, NPAIR * 16)

        @block.gpsimd
        def _(pool):
            pool.memset(zeros[:, :], 0.0).then_inc(filled, 1)
            pool.memset(empty[:, :, 0:D], 0.0)
            pool.memset(empty[:, :, D:ROW], float(FAR)).then_inc(filled, 1)
            pool.memset(power[:, :], -0.5).then_inc(pool_set, 1)
            pool.memset(ones[:, :], 1.0).then_inc(pool_set, 1)
            pool.iota(iota_e[:, :], pattern=[[1, E]], base=0, channel_multiplier=0,
                      allow_small_or_imprecise_dtypes=True).then_inc(pool_set, 1)
            pool.iota(place[:, :, :], pattern=[[2 * P, NT], [1, 2]], base=0, channel_multiplier=2,
                      allow_small_or_imprecise_dtypes=True).then_inc(pool_set, 1)
            pool.memset(sends[0][:, :, :, :], 0.0).then_inc(send_set, 1)
            pool.wait_ge(pool_set, 4)
            pool.affine_select(out=before[:, :], in_=ones[:, :], compare_op=ALU.is_gt, fill=0.0, base=0,
                               pattern=[[1, P]], channel_multiplier=-1).then_inc(pool_set, 1)
            att_rows = att[:, :, :, :, :].rearrange("p m h t d -> p t (m h) d")
            x_rows = x[:, :, :].rearrange("p t (m d) -> p t m d", d=DH)

            def send_rows(b, tiles):
                w = which(b)[0]
                for t in tiles:
                    for k in range(2):
                        pool.indirect_dma_start(
                            slots_in, bass.IndirectOffsetOnAxis(ap=send_to[w][:, t, k:k + 1], axis=0),
                            sends[w][:, t, k, :], None, bounds_check=E * CAP - 1, oob_is_err=False).then_inc(sent, 16)

            def route(b, r, part=0):
                if part > 0:
                    return
                last = which(b)[0] == 1
                if r == 0 and last:
                    wait_apart(pool, send_ready, b + 1, passed2)
                    send_rows(b - 1, range(0, 2))
                if r == 0:
                    wait_apart(pool, result_taken, b * TB + (TB + 1), passed2)
                    xb = x_rows[:, bass.ds(b * TB, TB), :, :]
                    pool.tensor_tensor(xb, xb, att_rows[:, :, bass.ds(b * H, H), :], ALU.add).then_inc(result_added, 1)
                    if not last:
                        pool.wait_ge(send_set, 1)
                        pool.wait_ge(slots_filled, SFILLS * 16)
                        wait_apart(pool, send_ready, b + 1, passed2)
                        send_rows(b - 1, range(TB))
                if r == 1:
                    pool.wait_ge(veps_ready, b + 1)
                    pool.tensor_tensor(rstd[:, :], veps[:, :], power[:, :], ALU.pow).then_inc(rstd_ready, 1)
                    if last:
                        send_rows(b - 1, range(2, 4))
                if r == 3:
                    pool.wait_ge(meps_ready, b + 1)
                    pool.tensor_tensor(rs[:, :], meps[:, :], power[:, :], ALU.pow).then_inc(rs_ready, 1)
                    xf = x[:, bass.ds(b * TB, TB), :]
                    pool.tensor_tensor(xf, xf, which(b)[2], ALU.add).then_inc(base_ready, 1)
                    if last:
                        send_rows(b - 1, range(4, TB))

            def step(s, u, rnd, what):
                if what is not None:
                    route(*what)
                if has(s, 1):
                    if not isinstance(s, int) or s > 0:
                        wait_apart(pool, av_done, s * TB, passed)
                    pool.tensor_copy(vb[:, (u + 1) % 2, :, :, :], v_all[:, bass.ds(s + 1, 1), :, :, :]).then_inc(v_ready, 1)
                if has(s, 2):
                    pool.wait_ge(scores_reduced, s * (2 * TB) + 3 * 2 * TB)
                    if not isinstance(s, int) or s > -2:
                        wait_apart(pool, misc_ready, s + 2, passed)
                    m = nmax[:, u % 2, :].rearrange("p (h t) -> p h t", h=2)
                    r = nrest[:, :, :].rearrange("p a (h t) -> p a h t", h=2)
                    def split_step(k, ins):
                        ins.then_inc(pool_own, 1)
                        wait_apart(pool, pool_own, s * 4 + (8 + k + 1), passed)

                    split_step(0, pool.tensor_copy(nparts[:, :, 0, :], m))
                    split_step(1, pool.tensor_tensor(r[:, 0], m, nparts[:, :, 0, :], ALU.subtract))
                    split_step(2, pool.tensor_copy(nparts[:, :, 1, :], r[:, 0]))
                    split_step(3, pool.tensor_tensor(r[:, 1], r[:, 0], nparts[:, :, 1, :], ALU.subtract))
                    pool.tensor_copy(nparts[:, :, 2, :], r[:, 1]).then_inc(nparts_ready, 1)
            steps(pool, step, route)
            pool.wait_ge(send_ready, B + 1)
            send_rows(B - 1, range(TB))
            pool.wait_ge(sent, (B + 1) * TB * 2 * 16)

        @block.scalar
        def _(act):
            def route(b, r, t):
                w, send, x2 = which(b)
                if r == 2:
                    if t == 0:
                        act.wait_ge(x2_ready, b + 1)
                    ins = act.activation(junk[:, t, :], x2[:, t, :], ACT.Square, accum_out=ss[:, t:t + 1])
                    if t == TB - 1:
                        ins.then_inc(ss_ready, 1)
                    if t in (1, 6):
                        half = t // 4
                        act.wait_ge(side_ready, b * SIDE + (half + 1))
                        act.activation(x2T[:, half * HALF:(half + 1) * HALF], ps_m[:, :], ACT.Copy).then_inc(side_taken, 1)
                if r in (3, 4, 5) and t >= 6:
                    first, end = ROUTED[r]
                    got = ps_m[:, 0:(end - first) * RW].rearrange("p (t c) -> p t c", c=RW)
                    if t == 6:
                        act.wait_ge(side_ready, b * SIDE + r)
                        act.wait_ge(rs_ready, b + 1)
                    for c in ((0, 1) if t == 6 else range(2, end - first)):
                        act.activation(gu_all[:, bass.ds(b * TB + (first + c), 1), :], got[:, c, E:RW], ACT.Copy,
                                       scale=rs[:, first + c:first + c + 1])
                    if t == 7:
                        act.activation(logits[:, first:end, :], got[:, :, 0:E], ACT.Copy).then_inc(side_taken, 1)
                if r == 4 and t < 4:
                    ins = act.activation(send[:, 2 * t:2 * t + 2, 1, 0:D], x2[:, 2 * t:2 * t + 2, :], ACT.Copy)
                    if t == 3:
                        ins.then_inc(x2_copied, 1)
                if r == 6 and t == 3:
                    act.wait_ge(diff_ready, b + 1)
                    act.activation(expo[:, :, :], expo[:, :, :], ACT.Exp).then_inc(expo_ready, 1)
                if r == 6 and t == 6:
                    act.wait_ge(side_ready, b * SIDE + 6)
                    act.activation(counts[:, :], ps_m[:, 0:(TB + 1) * E], ACT.Copy).then_inc(side_taken, 1)

            def step(s, u, rnd, what):
                def copy_av():
                    if has(s, -1):
                        act.wait_ge(av_done, s * TB)
                        at_least(act, misc_ready, s)
                        act.activation(avs[:, :], ps_av[0:AVR, :], ACT.Copy).then_inc(av_copied, 1)
                if has(s, 0):
                    for t in range(TB):
                        if not isinstance(s, int) or TB * s + t - PRING >= 0:
                            act.wait_ge(av_done, s * TB + (t - PRING + 1))
                        for j in range(4):
                            if t == 0 and j == 3:
                                copy_av()
                            if j == 2 and what is not None:
                                route(*what, t)
                            act.wait_ge(keyed_ready, s * (4 * TB) + (4 * t + j + 1))
                            act.activation(prob[:, t % PRING, j, :], ps_t[:, j % 2, :], ACT.Exp,
                                           scale=SOFTMAX_SCALE).then_inc(prob_ready, 1)
                else:
                    copy_av()
                    if what is not None:
                        for t in range(TB):
                            route(*what, t)
            steps(act, step, route)

            def shared(g, w, rnd):
                if has_group(g, 1):
                    at_least(act, sh_gu_ready, g + 1)
                    act.activation(sh_gelu[:, :, :], gu_all[:, bass.ds((g + 1) * TG, TG), 0:F4],
                                   ACT.Gelu).then_inc(sh_gelu_ready, 1)
                if has_group(g, 0):
                    act.wait_ge(sh_turned, g + 1)
                    act.activation(sh_guT[:, w, :], ps_t[0:F4, w, :], ACT.Copy).then_inc(sh_guT_ready, 1)
                if has_group(g, -1):
                    act.wait_ge(sh_down, g)
                    act.wait_ge(sh_added, g)
                    act.activation(sh_x[:, :, :], ps_s[:, 1 - w, 0:HALF], ACT.Copy).then_inc(sh_x_ready, 1)
            shared_steps(act, shared)

        @block.vector
        def _(dve):
            dve.memset(ps_av[:, :], 0.0).then_inc(av_cleared, 1)
            dve.memset(carry[:, :], 0.0).then_inc(carry_set, 1)
            dve.memset(send_to[0][:, :, :], FAR).then_inc(send_ready, 1)
            dve.sem_inc(result_taken, 1)
            dve.sem_inc(side_taken, 1)
            LINKS = 13
            last_link = 0

            def link(ins):
                nonlocal last_link
                ins.then_inc(dve_own, 1)
                last_link = last_link % LINKS + 1

            def linked(b):
                dve.wait_ge(dve_own, b * LINKS + last_link)

            def route(b, r, k):
                w, send, x2 = which(b)
                at = bass.ds(b * TB, TB)
                if r == 0 and k >= TB:
                    if k == TB:
                        dve.wait_ge(result_added, b + 1)
                    ins = dve.bn_stats(stats[:, k - TB, :], x[:, bass.ds(b * TB + (k - TB), 1), :])
                    if k == 2 * TB - 1:
                        ins.then_inc(stats_done, 1)
                if r == 1 and k == 0:
                    wait_apart(dve, stats_done, b + 1, passed2)
                    for t in range(TB):
                        ins = dve.bn_aggr(mv[:, t, :], stats[:, t, :])
                    ins.then_inc(mv_ready, 1)
                if r == 1 and k == 1:
                    dve.wait_ge(mv_ready, b + 1)
                    dve.tensor_scalar(veps[:, :], mv[:, :, 1], LN_EPS, None, ALU.add).then_inc(veps_ready, 1)
                if r == 1 and 6 <= k < 6 + TB:
                    t = k - 6
                    if t == 0:
                        dve.wait_ge(rstd_ready, b + 1)
                        if w == 0:
                            dve.wait_ge(sent, b * (TB * 2 * 16) + TB * 2 * 16)
                    ins = dve.tensor_scalar(x2[:, t, :], x[:, bass.ds(b * TB + t, 1), :], mv[:, t, 0:1],
                                            rstd[:, t:t + 1], ALU.subtract, ALU.mult)
                    if t == TB - 1:
                        ins.then_inc(x2_ready, 1)
                if r == 3 and k == 0:
                    dve.wait_ge(ss_ready, b + 1)
                    dve.tensor_scalar(meps[:, :], ss[:, :], 1.0 / D, RMS_EPS, ALU.mult, ALU.add).then_inc(meps_ready, 1)
                if r == 6:
                    if k == 0:
                        dve.wait_ge(side_taken, b * SIDE + 6)
                        for t in range(TB):
                            if t == 0:
                                dve.sem_inc(passed2, 1)
                            ins = dve.max(ranked[:, t, :], logits[:, t, :])
                        link(ins)
                    if k == 1:
                        linked(b)
                        dve.tensor_tensor(expo[:, :, :], ranked[:, :, :], ranked[:, :, 0:1].broadcast_to((P, TB, E)),
                                          ALU.subtract).then_inc(diff_ready, 1)
                        for t in range(TB):
                            ins = dve.max_index(index[:, t, :], ranked[:, t, :], logits[:, t, :])
                        link(ins)
                    if k == 2:
                        linked(b)
                        link(dve.tensor_copy(chosen[:, :, :], index[:, :, 0:2]))
                    if k == 3:
                        linked(b)
                        for c in range(2):
                            ins = dve.tensor_tensor(
                                onehot[:, c, :, :],
                                iota_e[:, :].rearrange("p (a e) -> p a e", a=1).broadcast_to((P, TB, E)),
                                chosen[:, :, c:c + 1].broadcast_to((P, TB, E)), ALU.is_equal)
                        link(ins)
                    if k == 4:
                        linked(b)
                        dve.tensor_tensor(given[:, :, :], onehot[:, 0, :, :], onehot[:, 1, :, :],
                                          ALU.add).then_inc(given_ready, 1)
                if r == 7:
                    if k == 0:
                        dve.wait_ge(expo_ready, b + 1)
                        link(dve.tensor_reduce(total[:, :], expo[:, :, :], AX.X, ALU.add))
                    if k == 1:
                        linked(b)
                        link(dve.reciprocal(inv[:, :], total[:, :]))
                    if k == 2:
                        linked(b)
                        dve.wait_ge(x2_copied, b + 1)
                        dve.tensor_tensor(send[:, :, :, D + 1], expo[:, :, 0:2],
                                          inv[:, :].rearrange("p (t a) -> p t a", a=1).broadcast_to((P, TB, 2)), ALU.mult)
                        dve.wait_ge(side_taken, b * SIDE + 7)
                        link(dve.tensor_tensor(gpos[:, :, :], counts[:, 0:TB * E].rearrange("p (t e) -> p t e", e=E),
                                               carry[:, :].rearrange("p (a e) -> p a e", a=1).broadcast_to((P, TB, E)),
                                               ALU.add))
                    if k == 3:
                        linked(b)
                        dve.tensor_tensor(carry[:, :], counts[:, TB * E:(TB + 1) * E], carry[:, :], ALU.add)
                        for c in range(2):
                            ins = dve.tensor_tensor(mpos[:, c, :, :], gpos[:, :, :], onehot[:, c, :, :], ALU.mult)
                        link(ins)
                    if k == 4:
                        linked(b)
                        link(dve.tensor_reduce(pos[:, :, :].rearrange("p t k -> p k t"), mpos[:, :, :, :], AX.X, ALU.add))
                    if k == 5:
                        linked(b)
                        link(dve.tensor_scalar(keep[:, :, :], pos[:, :, :], float(CAP), None, ALU.is_lt))
                    if k == 7:
                        linked(b)
                        dve.tensor_tensor(both[:, :], keep[:, :, 0], keep[:, :, 1], ALU.mult)
                        dve.tensor_scalar(far[:, :, :], keep[:, :, :], -float(FAR), float(FAR), ALU.mult, ALU.add)
                        link(dve.scalar_tensor_tensor(out=slot[:, :, :], in0=chosen[:, :, :], scalar=float(CAP),
                                                      in1=pos[:, :, :], op0=ALU.mult, op1=ALU.add))
                    if k == 8:
                        linked(b)
                        link(dve.tensor_scalar(overflow[:, at], both[:, :], -float(FAR), float(FAR), ALU.mult, ALU.add))
                    if k == 9:
                        linked(b)
                        link(dve.tensor_tensor(send[:, :, :, D].bitcast(U32), place[:, at, :],
                                               overflow[:, at].rearrange("p (t a) -> p t a", a=1).broadcast_to((P, TB, 2)),
                                               ALU.add))
                        dve.tensor_tensor(send_to[w][:, :, :], slot[:, :, :], far[:, :, :], ALU.add).then_inc(send_ready, 1)

            def misc(s, u, rnd, part):
                if part > 0:
                    if has(s, -1):
                        if part == 1:
                            dve.wait_ge(rden_ready, s)
                        hd = part - 1
                        for half in range(2):
                            j = 2 * hd + half
                            ins = dve.tensor_tensor(
                                att[:, bass.ds(s - 1, 1), hd, half * (TB // 2):(half + 1) * (TB // 2), :],
                                M_AV[:, :, 32 * j:32 * j + DH], rden4[:, :, j:j + 1].broadcast_to((P, 4, DH)), ALU.mult)
                        if part == 2:
                            ins.then_inc(result_taken, 1)
                    return
                dve.wait_ge(misc_ready, s + 2)
                if has(s, 1):
                    if not isinstance(s, int) or s >= 0:
                        dve.wait_ge(shifts_in[u], rnd * 32 + 32)
                    dve.tensor_copy(shift_rows[:, :], M_NM).then_inc(rows_copied, 1)
                if has(s, -1):
                    dve.reciprocal(rden4, M_AV[:, :, DH::32]).then_inc(rden_ready, 1)

            rden4 = rden[:, :, :].rearrange("p t h -> p (t h)").rearrange("p (c j) -> p c j", j=4)

            def step(s, u, rnd, what):
                if has(s, 2):
                    at_least(dve, nparts_ready, s + 1 if not isinstance(s, int) or s > 0 else 0)
                    for k in range(2 * TB):
                        if k in (6, 7, 8) and not (isinstance(s, int) and s < -1):
                            misc(s, u, rnd, k - 6)
                        if what is not None:
                            route(*what, k)
                        if k == 9 and isinstance(s, int) and s == 0:
                            dve.wait_ge(norms_ps, 1)
                            dve.tensor_copy(norms[:, :], ps_m[:, 0:E + 1]).then_inc(norms_ready, 1)
                            dve.wait_ge(w_in, 6 * 16)
                            dve.wait_ge(norms_ready, 1)
                            dve.tensor_scalar(rw[:, E:RW], fw_rows[:, :], norms[:, E:E + 1], None,
                                              ALU.mult).then_inc(rw_ready, 1)
                        dve.wait_ge(scores_ready, s * (2 * TB) + (4 * TB + k + 1))
                        dve.tensor_reduce(nmax[:, u % 2, k:k + 1], ps_s[:, k % 2, :], AX.X, ALU.max,
                                          negate=True).then_inc(scores_reduced, 1)
                else:
                    if what is not None:
                        for k in range(2 * TB):
                            route(*what, k)
                    for part in range(3):
                        misc(s, u, rnd, part)
            dve.wait_ge(pool_set, 4)
            dve.wait_ge(carry_set, 1)
            steps(dve, step, route, 2 * TB)

            def per_row(ap):
                return ap.rearrange("p (t a) -> p t a", a=1).broadcast_to((P, TG, D))

            def shared(g, w, rnd):
                if has_group(g, 1):
                    dve.wait_ge(sh_gelu_ready, g + 2)
                    at_least(dve, sh_turned, g + 1)
                    dve.tensor_tensor(sh_gu[:, :, :], sh_gelu[:, :, :], gu_all[:, bass.ds((g + 1) * TG, TG), F4:2 * F4],
                                      ALU.mult).then_inc(sh_gu_ready, 1)
                if has_group(g, -1):
                    dve.wait_ge(sh_added, g)
                    dve.tensor_scalar(room[:, :], overflow[:, bass.ds((g - 1) * TG, TG)], 0.0, None,
                                      ALU.is_equal).then_inc(room_ready, 1)
                    dve.wait_ge(sh_x_ready, g)
                    wait_apart(dve, room_ready, g, passed2)
                    dve.copy_predicated(sh_x[:, :, :], per_row(room[:, :].bitcast(U32)),
                                        zeros[:, 0:D].rearrange("p (a d) -> p a d", a=1).broadcast_to((P, TG, D))
                                        ).then_inc(sh_masked, 1)
                    xt = x[:, bass.ds((g - 1) * TG, TG), :]
                    dve.wait_ge(sh_masked, g)
                    dve.tensor_tensor(xt, xt, sh_x[:, :, :], ALU.add).then_inc(sh_added, 1)
            dve.wait_ge(base_ready, B)
            dve.sem_inc(sh_added, 1)
            shared_steps(dve, shared)

        @block.tensor
        def _(pe):

            def scores(s, u, k, n):
                w = (u + 2) % QBUF
                hd, t = k // TB, k % TB
                if n == 0 and (not isinstance(s, int) or s > -2 or k >= 2):
                    pe.wait_ge(scores_reduced, s * (2 * TB) + (4 * TB + k - 1))
                ins = pe.matmul(ps_s[:, k % 2, n * HALF:(n + 1) * HALF], qo[w][0:SHIFT, hd, t * P:(t + 1) * P],
                                ko[w][0:SHIFT, hd, n * HALF:(n + 1) * HALF], start=True, stop=True)
                if n == 1:
                    ins.then_inc(scores_ready, 1)

            def keyed(s, u, t, j):
                hd, half = j // 2, j % 2
                if not isinstance(s, int) or s > 0 or 4 * t + j >= 2:
                    pe.wait_ge(prob_ready, s * (4 * TB) + (4 * t + j - 1))
                pe.matmul(ps_t[:, j % 2, :], ko[u][0:KROWS, hd, t * P:(t + 1) * P],
                          qo[u][0:KROWS, hd, half * HALF:(half + 1) * HALF], start=True, stop=True).then_inc(keyed_ready, 1)

            def values(s, u, t):
                pe.wait_ge(prob_ready, s * (4 * TB) + (4 * t + 4))
                if t == 0:
                    pe.wait_ge(v_ready, s + 1)
                    at_least(pe, av_copied, s)
                for j in range(4):
                    ins = pe.matmul(ps_av[32 * j:32 * j + DH + 1, :], vb[:, u % 2, t, j // 2, :],
                                    prob[:, t % PRING, j, :], start=(t == 0), stop=(t == TB - 1))
                ins.then_inc(av_done, 1)

            def side_turns(b, r, t):
                before_it = max(r - 1, 0) if r != 2 else min(t, 1)
                return b * SIDE + (before_it + 1)

            def has_turn(r, t):
                return r == 2 and t == 0 or 2 <= r <= 6 and t == 5

            def route(b, r, t):
                w, send, x2 = which(b)
                if not has_turn(r, t):
                    return
                pe.wait_ge(side_taken, side_turns(b, r, t))
                if r == 2:
                    wait_apart(pe, x2_ready, b + 1, passed2)
                    half = t // 4
                    for c in range(4):
                        ins = pe.transpose(ps_m[:, c * P:(c + 1) * P], x2[:, 4 * half + c, :], ident[:, :])
                elif r < 6:
                    first, end = ROUTED[r]
                    for c in range(end - first):
                        tile = first + c
                        ins = pe.matmul(ps_m[:, c * RW:(c + 1) * RW], x2T[:, tile * P:(tile + 1) * P], rw[:, :],
                                        start=True, stop=True)
                else:
                    pe.wait_ge(given_ready, b + 1)
                    pe.matmul(ps_m[:, 0:TB * E], before[:, :], given[:, :, :], start=True, stop=False,
                              skip_group_check=True)
                    for j in range(TB):
                        ins = pe.matmul(ps_m[:, (j + 1) * E:(TB + 1) * E].rearrange("p (t e) -> p t e", e=E), ones[:, :],
                                        given[:, j:j + 1, :].broadcast_to((P, TB - j, E)), start=False,
                                        stop=(j == TB - 1), skip_group_check=True)
                ins.then_inc(side_ready, 1)

            def misc(s, u, what):
                if isinstance(s, int) and s == -1:
                    pe.wait_ge(pool_set, 5)
                if has(s, 0):
                    at_least(pe, rows_copied, s + 1)
                if has(s, -2):
                    pe.wait_ge(result_taken, s)
                if not isinstance(s, int) or s > 0:
                    pe.wait_ge(rw_ready, 1)
                if what is not None:
                    pe.wait_ge(side_taken, side_turns(*what, 2))
                if has(s, 1):
                    pe.wait_ge(nparts_ready, s + 2)
                if has(s, -1):
                    pe.wait_ge(av_copied, s)
                    for c in range(4):
                        ins = pe.transpose(M_AV[:, c, :], avs[:, c * P:(c + 1) * P], ident[0:AVR, 0:AVR])
                if has(s, 1):
                    ins = pe.transpose(M_NM, nparts[:, :, :, :].rearrange("p h a t -> p (h a t)"), identb[:, :])
                ins.then_inc(misc_ready, 1)

            def step(s, u, rnd, what):
                if has(s, 2):
                    w = (u + 2) % QBUF
                    pe.wait_ge(loads[w], (rnd + (u + 2) // QBUF) * 192 + 192)
                if has(s, 0):
                    pe.wait_ge(shifts_in[u], rnd * 32 + 32)
                for t in range(TB):
                    if has(s, 0):
                        keyed(s, u, t, 0)
                    if has(s, 2):
                        scores(s, u, 2 * t, 0)
                        scores(s, u, 2 * t, 1)
                        scores(s, u, 2 * t + 1, 0)
                    if has(s, 0):
                        keyed(s, u, t, 1)
                    if has(s, 2):
                        scores(s, u, 2 * t + 1, 1)
                    if has(s, 0):
                        keyed(s, u, t, 2)
                    if t > 0 and has(s, 0):
                        values(s, u, t - 1)
                    elif t == 0 and has(s, -1):
                        values(s - 1, (u + 3) % QBUF, TB - 1)
                    if has(s, 0):
                        keyed(s, u, t, 3)
                    if t == 2 and not (isinstance(s, int) and s < -1):
                        misc(s, u, what)
                    if what is not None and has_turn(what[1], t):
                        if has(s, 1):
                            at_least(pe, rows_copied, s + (2 if t > 2 else 1))
                        pe.wait_ge(result_taken, s + (1 if t > 2 else 0))
                        route(*what, t)
                    if t == 3 and isinstance(s, int) and s == 0:
                        pe.wait_ge(w_in, 6 * 16)
                        pe.wait_ge(rows_copied, 2)
                        pe.transpose(ps_m[:, 0:E + 1], norm_rows[:, :], ident[0:E + 1, 0:E + 1]).then_inc(norms_ps, 1)
            pe.wait_ge(av_cleared, 1)
            steps(pe, step, route)

            def shared(g, w, rnd):
                if has_group(g, 0):
                    wait_apart(pe, sh_gu_ready, g + 1, passed2)
                    for t in range(TG):
                        ins = pe.transpose(ps_t[0:F4, w, t * P:(t + 1) * P], sh_gu[:, t, :], ident[:, :])
                    ins.then_inc(sh_turned, 1)
                if has_group(g, -1):
                    pe.wait_ge(sh_guT_ready, g)
                    for t in range(TG):
                        ins = pe.matmul(ps_s[:, 1 - w, t * P:(t + 1) * P], sh_guT[:, 1 - w, t * P:(t + 1) * P], fwd[:, :],
                                        start=True, stop=True)
                    ins.then_inc(sh_down, 1)
            shared_steps(pe, shared)


def phase_experts(nc, Wg, Wu, Wd, slots_in, tok_out, norms, ident):
    with ExitStack() as ctx:
        def sb(name, shape, dt):
            return ctx.enter_context(nc.sbuf_tensor(name, shape, dt))

        def ps(name, shape, dt):
            return ctx.enter_context(nc.psum_tensor(name, shape, dt))

        def sem(name):
            return ctx.enter_context(nc.semaphore(name))

        NB = 2
        wg = [sb(f"wg{w}", [P, F], F32) for w in range(NB)]
        wu = [sb(f"wu{w}", [P, F], F32) for w in range(NB)]
        wd = [sb(f"wd{w}", [P, FT, D], F32) for w in range(NB)]
        rows = sb("rows", [P, E, CT, ROW], F32)
        ysum = sb("ysum", [P, CT, D], F32)
        yrows = [sb(f"yrows{w}", [P, CT, D], F32) for w in range(NB)]
        yplace = [sb(f"yplace{w}", [P, CT], U32) for w in range(NB)]
        junk = sb("junk2", [P, CT, D], F32)
        ss = sb("ss2", [P, CT], F32)
        meps = sb("meps2", [P, CT], F32)
        rs = sb("rs2", [P, CT], F32)
        power = sb("power3", [P, CT], F32)
        h = sb("h", [P, CT, D], F32)
        hT = sb("hT", [P, NB, CAP], F32)
        gelu = sb("gelu2", [P, FT, CAP], F32)
        gu = sb("gu2", [P, NB, FT, CAP], F32)
        ps_h = ps("ps_h", [P, CAP], F32)
        ps_g = ps("ps_g", [P, FT, CAP], F32)
        ps_u = ps("ps_u", [P, FT, CAP], F32)
        ps_y = ps("ps_y", [P, CT, D], F32)

        w_in = [sem(f"e_w_in{w}") for w in range(NB)]
        wd_in = [sem(f"e_wd_in{w}") for w in range(NB)]
        rows_in = [sem(f"e_rows_in{w}") for w in range(NB)]
        moved = [sem(f"e_moved{w}") for w in range(NB)]
        power_set = sem("e_power_set")
        ss_ready = sem("e_ss_ready")
        meps_ready = sem("e_meps_ready")
        rs_ready = sem("e_rs_ready")
        h_ready = sem("e_h_ready")
        turned = sem("e_turned")
        hT_ready = sem("e_hT_ready")
        gate_ps = sem("e_gate_ps")
        up_ps = sem("e_up_ps")
        gelu_ready = sem("e_gelu_ready")
        gu_ready = sem("e_gu_ready")
        down_ps = sem("e_down_ps")
        ysum_ready = sem("e_ysum_ready")
        y_ready = sem("e_y_ready")
        passed = sem("e_passed")

        block = ctx.enter_context(nc.Block())

        def steps(eng, step):
            run_steps(eng, step, -2, 1, 4, E + 1, NB)

        def has(s, offset):
            return has_item(s, offset, E)

        @block.sync
        def _(sp):
            def load_rows(e, w):
                sp.dma_start(rows[:, bass.ds(e, 1), :, :],
                             slots_in[bass.ds(e * CAP, CAP), :].rearrange("(t p) h -> p t h", p=P)).then_inc(rows_in[w], 16)

            def step(s, u, rnd):
                if has(s, 3) and not (isinstance(s, int) and s < -1):
                    sp.wait_ge(ss_ready, s + 2)
                    load_rows(s + 3, (u + 1) % NB)
                if has(s, 1):
                    w = (u + 1) % NB
                    at_least(sp, up_ps, s)
                    e = bass.ds(s + 1, 1)
                    sp.dma_start(wg[w][:, :], Wg[e, :, :].rearrange("a h f -> h (a f)")).then_inc(w_in[w], 16)
                    sp.dma_start(wu[w][:, :], Wu[e, :, :].rearrange("a h f -> h (a f)")).then_inc(w_in[w], 16)
                    at_least(sp, down_ps, s)
                    sp.dma_start(wd[w][:, :, :], Wd[e, :, :].rearrange("a (t p) h -> p (a t) h", p=P)).then_inc(wd_in[w], 16)
            steps(sp, step)

        @block.gpsimd
        def _(pool):
            pool.memset(power[:, :], -0.5).then_inc(power_set, 1)
            pool.wait_ge(power_set, 1)
            for w in range(NB):
                pool.dma_start(rows[:, w, :, :], slots_in[w * CAP:(w + 1) * CAP, :].rearrange("(t p) h -> p t h", p=P)
                               ).then_inc(moved[w], 16)

            def step(s, u, rnd):
                if has(s, 2):
                    pool.wait_ge(meps_ready, s + 3)
                    pool.tensor_tensor(rs[:, :], meps[:, :], power[:, :], ALU.pow).then_inc(rs_ready, 1)
                if has(s, -1):
                    w = (u + 1) % NB
                    wait_apart(pool, y_ready, s + 1, passed)
                    for t in range(CT):
                        pool.indirect_dma_start(
                            tok_out, bass.IndirectOffsetOnAxis(ap=yplace[w][:, t:t + 1], axis=0), yrows[w][:, t, :],
                            None, bounds_check=2 * N - 1, oob_is_err=False).then_inc(moved[w], 16)
            steps(pool, step)
            for w in range(NB):
                pool.wait_ge(moved[w], E // NB * CT * 16 + 16)

        @block.scalar
        def _(act):
            def step(s, u, rnd):
                if has(s, 0):
                    act.wait_ge(gate_ps, s + 1)
                    at_least(act, gu_ready, s)
                    act.activation(gelu[:, :, :], ps_g[:, :, :], ACT.Gelu).then_inc(gelu_ready, 1)
                if has(s, 2):
                    if isinstance(s, int) and s < 0:
                        act.wait_ge(moved[u], 16)
                    else:
                        act.wait_ge(rows_in[u], rnd * 16 + 16)
                    at_least(act, meps_ready, s + 2)
                    for t in range(CT):
                        ins = act.activation(junk[:, t, :], rows[:, bass.ds(s + 2, 1), t, 0:D], ACT.Square,
                                             accum_out=ss[:, t:t + 1])
                    ins.then_inc(ss_ready, 1)
                if has(s, 1):
                    act.wait_ge(turned, s + 2)
                    act.activation(hT[:, (u + 1) % NB, :], ps_h[:, :], ACT.Copy,
                                   scale=norms[:, bass.ds(s + 1, 1)]).then_inc(hT_ready, 1)
            steps(act, step)

        @block.vector
        def _(dve):
            dve.sem_inc(y_ready, 1)

            def per_slot(ap):
                return ap.broadcast_to((P, CT, D))

            def step(s, u, rnd):
                if has(s, 1):
                    dve.wait_ge(rs_ready, s + 2)
                    at_least(dve, turned, s + 1)
                    dve.tensor_tensor(h[:, :, :], rows[:, bass.ds(s + 1, 1), :, 0:D],
                                      per_slot(rs[:, :].rearrange("p (t a) -> p t a", a=1)), ALU.mult).then_inc(h_ready, 1)
                if has(s, 2):
                    dve.wait_ge(ss_ready, s + 3)
                    dve.tensor_scalar(meps[:, :], ss[:, :], 1.0 / D, RMS_EPS, ALU.mult, ALU.add).then_inc(meps_ready, 1)
                if has(s, 0):
                    dve.wait_ge(gelu_ready, s + 1)
                    dve.wait_ge(up_ps, s + 1)
                    dve.tensor_tensor(gu[:, u, :, :], gelu[:, :, :], ps_u[:, :, :], ALU.mult).then_inc(gu_ready, 1)
                if has(s, -1):
                    w = (u + 1) % NB
                    e = bass.ds(s - 1, 1)
                    dve.wait_ge(down_ps, s)
                    dve.tensor_tensor(ysum[:, :, :], ps_y[:, :, :], rows[:, e, :, 0:D], ALU.add).then_inc(ysum_ready, 1)
                    dve.wait_ge(moved[w], (rnd + ((u + 1) // NB - 1)) * (CT * 16) + 16)
                    dve.tensor_copy(yplace[w][:, :], rows[:, e, :, D].bitcast(U32))
                    dve.wait_ge(ysum_ready, s)
                    dve.tensor_tensor(yrows[w][:, :, :], ysum[:, :, :], per_slot(rows[:, e, :, D + 1].rearrange("p a t -> p t a")),
                                      ALU.mult).then_inc(y_ready, 1)
            steps(dve, step)

        @block.tensor
        def _(pe):
            def step(s, u, rnd):
                if has(s, 0):
                    pe.wait_ge(w_in[u], rnd * 32 + 32)
                    at_least(pe, gelu_ready, s)
                    pe.wait_ge(hT_ready, s + 1)
                    for f in range(FT):
                        ins = pe.matmul(ps_g[:, f, :], wg[u][:, f * P:(f + 1) * P], hT[:, u, :], start=True, stop=True)
                    ins.then_inc(gate_ps, 1)
                if has(s, 0):
                    at_least(pe, gu_ready, s)
                    for f in range(FT):
                        ins = pe.matmul(ps_u[:, f, :], wu[u][:, f * P:(f + 1) * P], hT[:, u, :], start=True, stop=True)
                    ins.then_inc(up_ps, 1)
                if has(s, 1):
                    wait_apart(pe, h_ready, s + 2, passed)
                    for t in range(CT):
                        ins = pe.transpose(ps_h[:, t * P:(t + 1) * P], h[:, t, :], ident[:, :])
                    ins.then_inc(turned, 1)
                if has(s, -1):
                    w = (u + 1) % NB
                    pe.wait_ge(wd_in[w], (rnd + (u + 1) // NB) * 16)
                    pe.wait_ge(y_ready, s)
                    pe.wait_ge(gu_ready, s)
                    for t in range(CT):
                        for f in range(FT):
                            ins = pe.matmul(ps_y[:, t, :], gu[:, w, f, t * P:(t + 1) * P], wd[w][:, f, :],
                                            start=(f == 0), stop=(f == FT - 1))
                    ins.then_inc(down_ps, 1)
            steps(pe, step)


def phase_combine(nc, tok_out, x, out):
    with ExitStack() as ctx:
        def sb(name, shape, dt):
            return ctx.enter_context(nc.sbuf_tensor(name, shape, dt))

        def sem(name):
            return ctx.enter_context(nc.semaphore(name))

        TG = 4
        NG = NT // TG
        got = [sb(f"got{g}", [P, TG, 2, D], F32) for g in range(NG)]
        both_in = [sem(f"both_in{g}") for g in range(NG)]
        first_added = sem("first_added")
        rows_ready = sem("rows_ready")
        written = sem("written")

        block = ctx.enter_context(nc.Block())

        @block.sync
        def _(sp):
            for g in range(NG):
                first = g * TG * P * 2
                sp.dma_start(got[g][:, :, :, :].rearrange("p t k d -> p t (k d)"),
                             tok_out[first:first + TG * P * 2, :].rearrange("(t p k) d -> p t (k d)", p=P, k=2)
                             ).then_inc(both_in[g], 16)

        @block.vector
        def _(dve):
            for g in range(NG):
                xg = x[:, g * TG:(g + 1) * TG, :]
                dve.wait_ge(both_in[g], 16)
                dve.tensor_tensor(xg, xg, got[g][:, :, 0, :], ALU.add).then_inc(first_added, 1)
                dve.wait_ge(first_added, g + 1)
                dve.tensor_tensor(xg, xg, got[g][:, :, 1, :], ALU.add).then_inc(rows_ready, 1)

        @block.scalar
        def _(act):
            for g in range(NG):
                act.wait_ge(rows_ready, g + 1)
                b, t = g * TG // TB, g * TG % TB
                act.dma_start(out[b, t * P:(t + TG) * P, :].rearrange("(t p) d -> p t d", p=P),
                              x[:, g * TG:(g + 1) * TG, :]).then_inc(written, 16)
            act.wait_ge(written, NG * 16)


_INS = ['L0_attn_z', 'L0_attn_W_qkv', 'L0_ffn_Wr', 'L0_ffn_norm_w', 'L0_ffn_Wg', 'L0_ffn_Wu', 'L0_ffn_Wd',
        'L0_ffn_f_norm', 'L0_ffn_fWg', 'L0_ffn_fWu', 'L0_ffn_fWd']
_OUTS = [((B, S, D), 'float32')]


def kernel(**inputs):
    import numpy as _np
    import concourse.bacc as _bacc
    from concourse import mybir as _mybir
    from concourse.bass_utils import run_bass_kernel_spmd as _run

    nc = _bacc.Bacc("TRN2", target_bir_lowering=False, num_devices=1)
    arrays, args = {}, []
    for name in _INS:
        a = _np.ascontiguousarray(inputs[name])
        arrays[f"in_{name}_dram"] = a
        args.append(nc.dram_tensor(f"in_{name}_dram", a.shape, _mybir.dt.from_np(a.dtype), kind="ExternalInput").ap())
    for i, (shape, dtype) in enumerate(_OUTS):
        dt = _mybir.dt.from_np(_np.dtype(dtype))
        args.append(nc.dram_tensor(f"out_{i}_dram", shape, dt, kind="ExternalOutput").ap())
    attention_moe(nc, *args)
    r = _run(nc, [arrays], core_ids=[0])
    return r.results[0]["out_0_dram"]
```
